# Optimizing a Trainium2 kernel written in Bass

```python
import numpy as np
import jax
import jax.numpy as jnp

def _softmax(x, axis=-1):
    return jax.nn.softmax(x, axis=axis)

def _gelu(x):
    return jax.nn.gelu(x, approximate=True)

def _silu(x):
    return jax.nn.silu(x)

def _sigmoid(x):
    return jax.nn.sigmoid(x)

def _layernorm(x, axis=-1, eps=1e-05):
    m = jnp.mean(x, axis=axis, keepdims=True)
    v = jnp.var(x, axis=axis, keepdims=True)
    return (x - m) / jnp.sqrt(v + eps)

def _scatter_add(tgt, idx, src, axis=0):
    return tgt.at[idx].add(src)

def _segment_sum(src, seg, n):
    return jax.ops.segment_sum(src, seg, n)
kernel_name = 'mk_seq_preln_d1_jaxref_r4_bf00db'

def setup_inputs(seed: int=0):
    np.random.seed(seed)
    _w = jnp.asarray

    def _L0_attn_setup():
        import jax, jax.numpy as jnp
        import numpy as np
        D_MODEL = 256
        EXPAND = 2
        D_INNER = EXPAND * D_MODEL
        D_STATE = 16
        D_CONV = 4
        DT_RANK = D_INNER
        BATCH, SEQ = (2, 256)
        EPS = 1e-05

        def _rmsnorm(x, w):
            var = jnp.mean(jnp.square(x), axis=-1, keepdims=True)
            return x * jax.lax.rsqrt(var + EPS) * w

        def _forward(x, rms_w, W_in, conv_w, conv_b, W_x, W_dt, A_log, W_out):
            B, L, _ = x.shape
            residual = x
            xn = _rmsnorm(x, rms_w)
            xr = xn @ W_in
            xs, res = jnp.split(xr, 2, axis=-1)
            xc = jnp.transpose(xs, (0, 2, 1))
            xc = jnp.pad(xc, ((0, 0), (0, 0), (D_CONV - 1, 0)))
            xc = jax.lax.conv_general_dilated(xc, conv_w, window_strides=(1,), padding='VALID', dimension_numbers=('NCH', 'OIH', 'NCH'), feature_group_count=D_INNER)
            xc = xc + conv_b[None, :, None]
            xs = jax.nn.silu(jnp.transpose(xc, (0, 2, 1)))
            x_ssm = xs @ W_x
            dt, Bm, Cm = jnp.split(x_ssm, [D_INNER, D_INNER + D_STATE], axis=-1)
            dt = jax.nn.softplus(dt @ W_dt)
            A = -jnp.exp(A_log)
            A_disc = jnp.exp(A[None, None] * dt[..., None])
            Bx = dt[..., None] * Bm[:, :, None, :] * xs[..., None]

            def step(h, inp):
                Ad_t, Bx_t, C_t = inp
                h = Ad_t * h + Bx_t
                y = jnp.einsum('bdn,bn->bd', h, C_t)
                return (h, y)
            h0 = jnp.zeros((B, D_INNER, D_STATE), xs.dtype)
            _, ys = jax.lax.scan(step, h0, (jnp.transpose(A_disc, (1, 0, 2, 3)), jnp.transpose(Bx, (1, 0, 2, 3)), jnp.transpose(Cm, (1, 0, 2))))
            y = jnp.transpose(ys, (1, 0, 2))
            y = y * jax.nn.silu(res)
            out = y @ W_out
            return residual + out
        key = jax.random.key(seed)
        ks = jax.random.split(key, 9)
        s = 0.02
        return {'x': jax.random.normal(ks[0], (BATCH, SEQ, D_MODEL), jnp.float32), 'rms_w': jnp.ones((D_MODEL,), jnp.float32), 'W_in': jax.random.normal(ks[1], (D_MODEL, 2 * D_INNER), jnp.float32) * s, 'conv_w': jax.random.normal(ks[2], (D_INNER, 1, D_CONV), jnp.float32) * 0.2, 'conv_b': jax.random.normal(ks[3], (D_INNER,), jnp.float32) * 0.02, 'W_x': jax.random.normal(ks[4], (D_INNER, DT_RANK + 2 * D_STATE), jnp.float32) * s, 'W_dt': jax.random.normal(ks[5], (DT_RANK, D_INNER), jnp.float32) * s, 'A_log': jax.random.normal(ks[6], (D_INNER, D_STATE), jnp.float32), 'W_out': jax.random.normal(ks[7], (D_INNER, D_MODEL), jnp.float32) * s}
    _L0_attn_in = _L0_attn_setup()

    def _L0_ffn_setup():
        import jax, jax.numpy as jnp
        import numpy as np
        D_MODEL = 256
        D_FF = 704
        N_EXPERTS = 8
        key = jax.random.key(seed)
        k_in, k1, k2, k3 = jax.random.split(key, 4)
        scale = 0.02
        inputs = jax.random.normal(k_in, (4, N_EXPERTS * 512, D_MODEL), dtype=jnp.float32)
        w1 = jax.random.normal(k1, (N_EXPERTS, D_MODEL, D_FF), dtype=jnp.float32) * scale
        w3 = jax.random.normal(k3, (N_EXPERTS, D_MODEL, D_FF), dtype=jnp.float32) * scale
        w2 = jax.random.normal(k2, (N_EXPERTS, D_FF, D_MODEL), dtype=jnp.float32) * scale
        return {'inputs': inputs, 'w1': w1, 'w3': w3, 'w2': w2}
    _L0_ffn_in = _L0_ffn_setup()
    _d = {'L0_attn_x': _L0_attn_in['x'], 'L0_attn_rms_w': _L0_attn_in['rms_w'], 'L0_attn_W_in': _L0_attn_in['W_in'], 'L0_attn_conv_w': _L0_attn_in['conv_w'], 'L0_attn_conv_b': _L0_attn_in['conv_b'], 'L0_attn_W_x': _L0_attn_in['W_x'], 'L0_attn_W_dt': _L0_attn_in['W_dt'], 'L0_attn_A_log': _L0_attn_in['A_log'], 'L0_attn_W_out': _L0_attn_in['W_out'], 'L0_ffn_w1': _L0_ffn_in['w1'], 'L0_ffn_w3': _L0_ffn_in['w3'], 'L0_ffn_w2': _L0_ffn_in['w2']}
    _x0 = _d['L0_attn_x']
    _d['L0_attn_x'] = jax.random.normal(jax.random.fold_in(jax.random.key(seed), 1), (1, 4096, 256), dtype=_x0.dtype)
    del _x0
    return _d

def reference(L0_attn_x, L0_attn_rms_w, L0_attn_W_in, L0_attn_conv_w, L0_attn_conv_b, L0_attn_W_x, L0_attn_W_dt, L0_attn_A_log, L0_attn_W_out, L0_ffn_w1, L0_ffn_w3, L0_ffn_w2):

    def _L0_attn_ref(x, rms_w, W_in, conv_w, conv_b, W_x, W_dt, A_log, W_out):
        import jax, jax.numpy as jnp
        import numpy as np
        D_MODEL = 256
        EXPAND = 2
        D_INNER = EXPAND * D_MODEL
        D_STATE = 16
        D_CONV = 4
        DT_RANK = D_INNER
        BATCH, SEQ = (2, 256)
        EPS = 1e-05

        def _rmsnorm(x, w):
            var = jnp.mean(jnp.square(x), axis=-1, keepdims=True)
            return x * jax.lax.rsqrt(var + EPS) * w

        def _forward(x, rms_w, W_in, conv_w, conv_b, W_x, W_dt, A_log, W_out):
            B, L, _ = x.shape
            residual = x
            xn = _rmsnorm(x, rms_w)
            xr = xn @ W_in
            xs, res = jnp.split(xr, 2, axis=-1)
            xc = jnp.transpose(xs, (0, 2, 1))
            xc = jnp.pad(xc, ((0, 0), (0, 0), (D_CONV - 1, 0)))
            xc = jax.lax.conv_general_dilated(xc, conv_w, window_strides=(1,), padding='VALID', dimension_numbers=('NCH', 'OIH', 'NCH'), feature_group_count=D_INNER)
            xc = xc + conv_b[None, :, None]
            xs = jax.nn.silu(jnp.transpose(xc, (0, 2, 1)))
            x_ssm = xs @ W_x
            dt, Bm, Cm = jnp.split(x_ssm, [D_INNER, D_INNER + D_STATE], axis=-1)
            dt = jax.nn.softplus(dt @ W_dt)
            A = -jnp.exp(A_log)
            A_disc = jnp.exp(A[None, None] * dt[..., None])
            Bx = dt[..., None] * Bm[:, :, None, :] * xs[..., None]

            def step(h, inp):
                Ad_t, Bx_t, C_t = inp
                h = Ad_t * h + Bx_t
                y = jnp.einsum('bdn,bn->bd', h, C_t)
                return (h, y)
            h0 = jnp.zeros((B, D_INNER, D_STATE), xs.dtype)
            _, ys = jax.lax.scan(step, h0, (jnp.transpose(A_disc, (1, 0, 2, 3)), jnp.transpose(Bx, (1, 0, 2, 3)), jnp.transpose(Cm, (1, 0, 2))))
            y = jnp.transpose(ys, (1, 0, 2))
            y = y * jax.nn.silu(res)
            out = y @ W_out
            return residual + out
        return _forward(x, rms_w, W_in, conv_w, conv_b, W_x, W_dt, A_log, W_out)

    def _L0_ffn_ref(inputs, w1, w3, w2):
        import jax, jax.numpy as jnp
        import numpy as np
        D_MODEL = 256
        D_FF = 704
        N_EXPERTS = 8
        B, T, D = inputs.shape
        E = w1.shape[0]
        C = T // E
        x = inputs.reshape(B, E, C, D)
        gate = jnp.einsum('becd,edf->becf', x, w1)
        up = jnp.einsum('becd,edf->becf', x, w3)
        h = jax.nn.silu(gate) * up
        out = jnp.einsum('becf,efd->becd', h, w2)
        return out.reshape(B, T, D)
    x = L0_attn_x
    x = x + _L0_attn_ref(_layernorm(x, axis=-1), L0_attn_rms_w, L0_attn_W_in, L0_attn_conv_w, L0_attn_conv_b, L0_attn_W_x, L0_attn_W_dt, L0_attn_A_log, L0_attn_W_out)
    x = x + _L0_ffn_ref(_layernorm(x, axis=-1), L0_ffn_w1, L0_ffn_w3, L0_ffn_w2)
    return x

_drawn_inputs = setup_inputs


def setup_inputs(seed=0):
    import zlib

    import numpy as np

    out = dict(_drawn_inputs(seed))
    spreads = {'L0_attn_rms_w': (1.0, 0.2)}
    factors = {}
    for name, (base, spread) in spreads.items():
        noise = np.random.default_rng([zlib.crc32(name.encode()), seed]).standard_normal(out[name].shape)
        drawn = base * np.exp(spread * noise) if base else spread * noise
        out[name] = jnp.asarray(drawn.astype(out[name].dtype))
    for name, factor in factors.items():
        out[name] = (out[name] * factor).astype(out[name].dtype)
    return out
```

```python
import concourse.bass as bass
from concourse import mybir
from contextlib import ExitStack

f32 = mybir.dt.float32
bf16 = mybir.dt.bfloat16
ALU = mybir.AluOpType
ACT = mybir.ActivationFunctionType


def mamba_moe_layer(nc, x, rms_w, W_in, conv_w, conv_b, W_x, W_dt, A_log, W_out, w1, w3, w2, out):
    T, D = x.shape[1], x.shape[2]
    DI, N = A_log.shape
    TAPS = conv_w.shape[2]
    E, _, FF = w1.shape
    P = 128
    TC = T // E
    NT = TC // P
    KD = D // P
    ND = DI // P
    HALO = TAPS - 1
    NG = 4
    GPD = N // NG
    Q = ND * GPD
    NS = Q * NG
    RING = 3
    FT = FF // P
    FR = FF - FT * P
    assert FR * 2 == P and 3 * 2 * N == 96 and TC == 512
    EPS = 1e-5

    ctx = ExitStack()
    with ctx:
        def sb(name, shape, dt=f32):
            return ctx.enter_context(nc.sbuf_tensor(name, shape, dt))

        def pb(name):
            return ctx.enter_context(nc.psum_tensor(name, [P, TC], f32))

        def sem(name):
            return ctx.enter_context(nc.semaphore(name))

        b_all = sb("b_all", [P, N, TC])
        c_all = sb("c_all", [P, N, TC])
        ring = sb("ring", [P, RING, NG, TC])
        dt_ = sb("dt_", [P, ND, TC])
        xs = sb("xs", [P, ND, TC])
        sres = sb("sres", [P, ND, TC])
        xin = sb("xin", [P, NT, D])
        xres = sb("xres", [P, NT, D])
        xT = sb("xT", [P, KD, TC])
        xpre = sb("xpre", [P, ND, HALO + TC])
        hb = sb("hb", [P, FT + 1, TC])
        x1 = sb("x1", [P, NT, D])
        xn2 = sb("xn2", [P, NT, D])
        bc_r = sb("bc_r", [6 * N, TC])
        bc_s = sb("bc_s", [6 * N, TC], bf16)
        win = sb("win", [P, KD, 2 * DI])
        wc = sb("wc", [P, ND, DI])
        wbc = sb("wbc", [P, ND, 3, 2 * N])
        wout = sb("wout", [P, ND, D])
        cdiag = sb("cdiag", [P, ND, TAPS, P])
        w13 = sb("w13", [P, KD, 2, FT * P])
        w13t = sb("w13t", [P, KD, P])
        w2s = sb("w2s", [P, FT + 1, D])
        ident = sb("ident", [P, P])
        pick = sb("pick", [6 * N, 2 * N], bf16)
        a_neg = sb("a_neg", [P, ND, N])
        cw = sb("cw", [P, ND, TAPS])
        cb = sb("cb", [P, ND])
        rw = sb("rw", [P, KD])
        state = sb("state", [P, Q, NG])
        bn = sb("bn", [P, NT, 6])
        mv = sb("mv", [P, NT, 2])
        bn2 = sb("bn2", [P, NT, 6])
        mv2 = sb("mv2", [P, NT, 2])
        st = sb("st", [P, 12, NT])
        st2 = sb("st2", [P, 4, NT])
        consts = sb("consts", [P, 5, NT])
        taken = sb("taken", [1, 1])
        wx_ld = hb[:, :, :].rearrange("p a b -> p (a b)")[:, 0:ND * (DI + 2 * N)].rearrange("p (k n) -> p k n", k=ND)
        wxT = ring[:, 0, :, :]
        wdt_ld = ring[:, 1, :, :]

        ubank = pb("ubank")
        ybank = pb("ybank")
        ebank = [pb("ebank0"), pb("ebank1")]
        gbank = [pb(f"gbank{b}") for b in range(4)]
        NB = len(gbank)

        F_XT, F_IN, F_CONV, F_DT, F_BC, F_SPREAD = 0, KD, KD + 2 * ND, KD + 3 * ND, KD + 4 * ND, KD + 4 * ND + 1
        F_USES = F_SPREAD + 2 * N
        O_XT, O_GATE, O_TAIL, O_UP, O_DOWN = 0, KD, KD + FT, KD + FT + 1, KD + 2 * FT + 1
        O_USES = O_DOWN + NT // 2
        M_USES = NT // 2
        full = [sem(f"full{b}") for b in range(NB)]
        free = [sem(f"free{b}") for b in range(NB)]
        per = {s: [len(range(b, u, NB)) for b in range(NB)] for s, u in (("F", F_USES), ("O", O_USES), ("M", M_USES))}

        def nth(stage, c, k):
            b = k % NB
            f, o, m = per["F"][b], per["O"][b], per["M"][b]
            if stage == "F":
                before = 0 if isinstance(c, int) and c == 0 else c * (f + o + m) - o
            elif stage == "M":
                before = f if isinstance(c, int) and c == 0 else c * (f + o + m) + f
            else:
                last = isinstance(c, int) and c == E - 1
                before = (c + 1) * (f + o + m) - o + (0 if last else f)
            return b, before + k // NB + 1

        def wait_full(e, stage, c, k):
            b, n = nth(stage, c, k)
            e.wait_ge(full[b], n)
            return gbank[b]

        def wait_read(e, stage, c, k):
            b, n = nth(stage, c, k)
            e.wait_ge(free[b], n)

        def wait_free(e, stage, c, k):
            b, n = nth(stage, c, k)
            if not (isinstance(n, int) and n == 1):
                e.wait_ge(free[b], n - 1)
            return gbank[b]

        def filled(ins, k):
            ins.then_inc(full[k % NB], 1)

        def read_out(ins, k):
            ins.then_inc(free[k % NB], 1)

        events = []

        class Event:
            def __init__(self, name, number):
                self.sem, self.number = sem("s_" + name), number
                events.append(self)

            def wait(self, e, c, j=None):
                e.wait_ge(self.sem, (c + 1) * self.number + (self.number if j is None else j))

            def by(self, ins, n=1):
                ins.then_inc(self.sem, n)

        x_in, w13_in, w2_in, stored = (Event(n, k) for n, k in (("x_in", 16), ("w13_in", 64), ("w2_in", 32), ("stored", 16)))
        bn_ok = Event("bn_ok", 1)
        stats = Event("stats", 1)
        scales = Event("scales", 11)
        xres_ok = Event("xres_ok", NT)
        xn_ok = Event("xn_ok", NT)
        halo_ok = Event("halo_ok", 1)
        soft = Event("soft", 3 * ND)
        dt_ok = Event("dt_ok", ND)
        bc_ok = Event("bc_ok", 4)
        u_ok = Event("u_ok", ND)
        bu_ok = Event("bu_ok", Q)
        e_ok = Event("e_ok", NS)
        h_ok = Event("h_ok", NS)
        st_ok = Event("st_ok", Q)
        ch_ok = Event("ch_ok", Q)
        y_ok = Event("y_ok", Q)
        yg_ok = Event("yg_ok", ND)
        bn2_ok = Event("bn2_ok", 1)
        stats2 = Event("stats2", 1)
        scales2 = Event("scales2", 4)
        xn2_ok = Event("xn2_ok", NT)
        silu_ok = Event("silu_ok", 3)

        s_ld = [sem(f"s_ld{n}") for n in range(4)]
        s_id = sem("s_id")
        s_c = sem("s_c")
        s_ca = sem("s_ca")
        s_tr = sem("s_tr")
        s_tc = sem("s_tc")

        block = ctx.enter_context(nc.Block())

        def rows(t, c):
            return t[0, bass.ds(c * TC, TC), :].rearrange("(b p) d -> p b d", p=P)

        @block.sync
        def _(e):
            for ev in events:
                e.sem_inc(ev.sem, ev.number)

            def load_x(c):
                e.dma_start(xin[:, :, :], rows(x, c)).then_inc(x_in.sem, 16)

            def load_expert(c):
                if not (isinstance(c, int) and c == 0):
                    wait_full(e, "O", c - 1, O_UP + FT - 1)
                for j, w in enumerate((w1, w3)):
                    src = w[bass.ds(c, 1), :, :].rearrange("a (k p) f -> p (a k) f", p=P)
                    e.dma_start(w13[:, :, j, :], src[:, :, 0:FT * P]).then_inc(w13_in.sem, 16)
                    e.dma_start(w13t[:, :, j * FR:(j + 1) * FR], src[:, :, FT * P:FF]).then_inc(w13_in.sem, 16)
                if not (isinstance(c, int) and c == 0):
                    for t in range(NT // 2):
                        wait_full(e, "O", c - 1, O_DOWN + t)
                e.dma_start(w2s[:, 0:FT, :], w2[bass.ds(c, 1), 0:FT * P, :].rearrange("a (k p) d -> p (a k) d", p=P)).then_inc(w2_in.sem, 16)
                e.dma_start(w2s[P - FR:P, FT:FT + 1, :], w2[bass.ds(c, 1), FT * P:FF, :].rearrange("a p d -> p a d")).then_inc(w2_in.sem, 16)

            def store(c):
                for t in range(NT // 2):
                    wait_read(e, "O", c, O_DOWN + t)
                e.dma_start(rows(out, c), x1[:, :, :]).then_inc(stored.sem, 16)

            load_x(0)
            e.dma_start(cw[:, :, :], conv_w.rearrange("(d p) a k -> p d (a k)", p=P)).then_inc(s_ld[0], 16)
            e.dma_start(cb[:, :], conv_b.rearrange("(d p) -> p d", p=P), allow_slow_non_contiguous=True).then_inc(s_ld[0], 16)
            e.dma_start(rw[:, :], rms_w.rearrange("(d p) -> p d", p=P), allow_slow_non_contiguous=True).then_inc(s_ld[0], 16)
            e.dma_start(a_neg[:, :, :], A_log.rearrange("(d p) n -> p d n", p=P)).then_inc(s_ld[0], 16)
            e.dma_start(win[:, :, :], W_in.rearrange("(k p) n -> p k n", p=P)).then_inc(s_ld[3], 16)
            e.dma_start(wx_ld, W_x.rearrange("(k p) n -> p k n", p=P)).then_inc(s_ld[1], 16)
            e.dma_start(wdt_ld, W_dt.rearrange("(k p) n -> p k n", p=P)).then_inc(s_ld[2], 16)
            e.dma_start(wout[:, :, :], W_out.rearrange("(k p) n -> p k n", p=P)).then_inc(s_ld[3], 16)
            load_expert(0)

            def next_x(c):
                for k in range(KD):
                    wait_full(e, "F", c - 1, F_XT + k)
                load_x(c)

            next_x(1)
            with e.Fori(1, E - 1) as i:
                next_x(i + 1)
                store(i - 1)
                load_expert(i)
            store(E - 2)
            load_expert(E - 1)
            store(E - 1)
            stored.wait(e, E - 1)

        @block.gpsimd
        def _(e):
            made = [0]

            def step(ins):
                made[0] += 1
                ins.then_inc(s_id, 1)
                e.wait_ge(s_id, made[0])

            for n, value in enumerate((-0.5, EPS, -1.0, 1.0, 0.0)):
                step(e.memset(consts[:, n, :], value))
            step(e.memset(ident[:, :], 0.0))
            step(e.memset(pick[:, :], 0.0))
            step(e.memset(state[:, :, :], 0.0))
            step(e.memset(xpre[:, :, 0:HALO], 0.0))
            step(e.affine_select(out=ident[:, :], in_=ident[:, :], compare_op=ALU.not_equal, fill=1.0,
                                 base=0, pattern=[[-1, P]], channel_multiplier=1))
            for r in range(3):
                step(e.affine_select(out=pick[:, :], in_=pick[:, :], compare_op=ALU.not_equal, fill=1.0,
                                     base=-r * 2 * N, pattern=[[-1, 2 * N]], channel_multiplier=1))

            mhalf, eps, minus, one, zero = (consts[:, n, :] for n in range(5))

            def front(c):
                j = [0]

                def then(ins):
                    j[0] += 1
                    scales.by(ins)
                    scales.wait(e, c, j[0])

                m, v = mv[:, :, 0], mv[:, :, 1]
                ve, r, vr, ms, mse, r2, s, nm, bs, br, rp = (st[:, n, :] for n in range(11))
                stats.wait(e, c)
                xn_ok.wait(e, c - 1)
                then(e.tensor_tensor(ve, v, eps, ALU.add))
                then(e.tensor_tensor(r, ve, mhalf, ALU.pow))
                then(e.tensor_tensor(vr, v, r, ALU.mult))
                then(e.tensor_tensor(ms, vr, r, ALU.mult))
                then(e.tensor_tensor(mse, ms, eps, ALU.add))
                then(e.tensor_tensor(r2, mse, mhalf, ALU.pow))
                then(e.tensor_tensor(s, r, r2, ALU.mult))
                then(e.tensor_tensor(nm, m, minus, ALU.mult))
                then(e.tensor_tensor(bs, nm, s, ALU.mult))
                then(e.tensor_tensor(br, nm, r, ALU.mult))
                then(e.tensor_tensor(rp, r, one, ALU.add))

            def group(c, q):
                slot, g = ring[:, q % RING, :, :], q % GPD
                h_ok.wait(e, c, NG * (q + 1))
                st_ok.by(e.tensor_tensor(state[:, q, :], slot[:, :, TC - 1], zero, ALU.add))
                st_ok.wait(e, c, q + 1)
                if q < GPD:
                    for n in range(NG):
                        wait_read(e, "F", c, F_SPREAD + (2 * g + 1) * NG + n)
                ch_ok.by(e.tensor_tensor(slot, slot, c_all[:, g * NG:(g + 1) * NG, :], ALU.mult))

            def back(c):
                def then(ins, j):
                    scales2.by(ins)
                    scales2.wait(e, c, j)

                stats2.wait(e, c)
                xn2_ok.wait(e, c - 1)
                then(e.tensor_tensor(st2[:, 0, :], mv2[:, :, 1], eps, ALU.add), 1)
                then(e.tensor_tensor(st2[:, 1, :], st2[:, 0, :], mhalf, ALU.pow), 2)
                then(e.tensor_tensor(st2[:, 2, :], mv2[:, :, 0], minus, ALU.mult), 3)
                then(e.tensor_tensor(st2[:, 3, :], st2[:, 2, :], st2[:, 1, :], ALU.mult), 4)

            def iteration(i, with_back):
                front(i)
                for q in range(Q):
                    if with_back and q == 0:
                        back(i - 1)
                    group(i, q)

            iteration(0, False)
            with e.Fori(1, E) as i:
                iteration(i, True)
            back(E - 1)

        @block.vector
        def _(e):
            e.wait_ge(s_ld[0], 64)
            e.wait_ge(s_ld[3], 32)
            for k in range(KD):
                e.tensor_scalar(win[:, k, :], win[:, k, :], rw[:, k:k + 1], None, ALU.mult).then_inc(s_c, 1)
            e.wait_ge(s_id, 13)
            for d in range(ND):
                for k in range(TAPS):
                    e.tensor_scalar(cdiag[:, d, k, :], ident[:, :], cw[:, d, k:k + 1], None, ALU.mult).then_inc(s_c, 1)
            e.wait_ge(s_ld[1], 16)
            for r in range(3):
                e.tensor_copy(wbc[:, :, r, :], wx_ld[:, :, DI:DI + 2 * N]).then_inc(s_c, 1)
            for j in range(ND):
                e.wait_ge(s_tr, j + 1)
                e.tensor_copy(wxT[:, j, :], gbank[j][:, :]).then_inc(s_tc, 1)
            for k in range(ND):
                e.wait_ge(s_tr, ND + k + 1)
                e.tensor_copy(wc[:, k, :], gbank[k][:, :]).then_inc(s_tc, 1)

            def take():
                e.tensor_copy(taken[:, :], rw[0:1, 0:1])

            def front(c):
                x_in.wait(e, c)
                stats.wait(e, c - 1)
                scales.wait(e, c - 1)
                for b in range(NT):
                    last = e.bn_stats(bn[:, b, :], xin[:, b, :])
                bn_ok.by(last)
                bn_ok.wait(e, c)
                take()
                for b in range(NT):
                    last = e.bn_aggr(mv[:, b, :], bn[:, b, :])
                stats.by(last)
                bank = wait_full(e, "F", c, F_BC)
                w = 2 * N
                bc_ok.by(e.tensor_copy(bc_s[:, :], bank[0:3 * w, :]))
                bc_ok.wait(e, c, 1)
                read_out(e.tensor_tensor(bc_r[:, :], bank[0:3 * w, :], bc_s[:, :], ALU.subtract), F_BC)
                wait_read(e, "F", c, F_BC)
                for r in (1, 2):
                    bc_ok.by(e.tensor_copy(bc_s[r * w:(r + 1) * w, :], bc_r[r * w:(r + 1) * w, :]))
                bc_ok.wait(e, c, 3)
                third = slice(2 * w, 3 * w)
                bc_ok.by(e.tensor_tensor(bc_s[third, :], bc_r[third, :], bc_s[third, :], ALU.subtract))
                e_ok.wait(e, c - 1)
                for d in range(ND):
                    soft.wait(e, c, 3 * (d + 1))
                    dt_ok.by(e.tensor_tensor(dt_[:, d, :], xpre[:, d, HALO:HALO + TC], hb[:, d, :], ALU.add))
                bu_ok.wait(e, c - 1)
                for k in range(2 * N):
                    if k % (2 * NG) < NG:
                        n = k // (2 * NG) * NG + k % NG
                        bank = wait_full(e, "F", c, F_SPREAD + k)
                        read_out(e.tensor_copy(b_all[:, n, :], bank[:, :]), F_SPREAD + k)

            def u_of(c, d):
                dt_ok.wait(e, c, d + 1)
                bu_ok.wait(e, c, d * GPD)
                wait_read(e, "F", c, F_CONV + d)
                u_ok.by(e.tensor_tensor(ubank[:, :], dt_[:, d, :], xs[:, d, :], ALU.mult))

            def bu(c, q):
                g = q % GPD
                u_ok.wait(e, c, q // GPD + 1)
                if q >= RING:
                    y_ok.wait(e, c, q - RING + 1)
                else:
                    y_ok.wait(e, c - 1, (Q - 1 - q) // RING * RING + q + 1)
                if q < GPD:
                    for n in range(NG):
                        wait_read(e, "F", c, F_SPREAD + 2 * g * NG + n)
                bu_ok.by(e.tensor_tensor(ring[:, q % RING, :, :], b_all[:, g * NG:(g + 1) * NG, :],
                                         ubank[:, :].unsqueeze(1).broadcast_to([P, NG, TC]), ALU.mult))

            def scans(c, q):
                bu_ok.wait(e, c, q + 1)
                st_ok.wait(e, c - 1, q + 1)
                for n in range(NG):
                    j = q * NG + n
                    e_ok.wait(e, c, j + 1)
                    row = ring[:, q % RING, n, :]
                    h_ok.by(e.tensor_tensor_scan(row, ebank[j % 2][:, :], row, initial=state[:, q, n:n + 1],
                                                 op0=ALU.mult, op1=ALU.add))

            def gated(c, d):
                y_ok.wait(e, c, GPD * (d + 1))
                wait_read(e, "F", c, F_IN + ND + d)
                yg_ok.by(e.tensor_tensor(sres[:, d, :], ybank[:, :], sres[:, d, :], ALU.mult))

            def back_stats(c):
                for t in range(NT // 2):
                    wait_read(e, "M", c, t)
                stats2.wait(e, c - 1)
                scales2.wait(e, c - 1)
                for b in range(NT):
                    last = e.bn_stats(bn2[:, b, :], x1[:, b, :])
                bn2_ok.by(last)
                bn2_ok.wait(e, c)
                take()
                for b in range(NT):
                    last = e.bn_aggr(mv2[:, b, :], bn2[:, b, :])
                stats2.by(last)

            def hidden(c, f):
                part = slice(0, P) if f < FT else slice(FR, P)
                use = O_UP + f if f < FT else O_TAIL
                silu_ok.wait(e, c, 2 if f < FT else 3)
                bank = wait_full(e, "O", c, use)
                read_out(e.tensor_tensor(hb[part, f, :], hb[part, f, :], bank[part, :], ALU.mult), use)

            def result(c, t):
                bank = wait_full(e, "O", c, O_DOWN + t)
                xn2_ok.wait(e, c)
                two = x1[:, 2 * t:2 * t + 2, :]
                read_out(e.tensor_tensor(two, two, bank[:, :].rearrange("p (b d) -> p b d", b=2), ALU.add), O_DOWN + t)

            def project(c):
                stored.wait(e, c - 1)
                xres_ok.wait(e, c)
                for t in range(NT // 2):
                    bank = wait_full(e, "M", c, t)
                    two = slice(2 * t, 2 * t + 2)
                    read_out(e.tensor_tensor(x1[:, two, :], xres[:, two, :], bank[:, :].rearrange("p (b d) -> p b d", b=2), ALU.add), t)

            BACK = {0: (back_stats,), 9: (lambda c: hidden(c, FT), lambda c: hidden(c, 0)), 10: (lambda c: hidden(c, 1),),
                    11: (lambda c: hidden(c, 2),), 12: (lambda c: hidden(c, 3),), 13: (lambda c: hidden(c, 4),),
                    14: (lambda c: result(c, 0),), 15: (lambda c: result(c, 1),)}

            def iteration(i, with_back):
                front(i)
                u_of(i, 0)
                bu(i, 0)
                for q in range(Q):
                    d, g = q // GPD, q % GPD
                    scans(i, q)
                    if q + 1 < Q:
                        if g == GPD - 1:
                            u_of(i, d + 1)
                        bu(i, q + 1)
                    if with_back:
                        for job in BACK.get(q, ()):
                            job(i - 1)
                    if g == 0 and d:
                        gated(i, d - 1)
                gated(i, ND - 1)
                project(i)

            iteration(0, False)
            with e.Fori(1, E) as i:
                iteration(i, True)
            for q in range(Q):
                for job in BACK.get(q, ()):
                    job(E - 1)

        @block.scalar
        def _(e):
            LOG_EXP = "natural_log_exp_and_others"
            e.preload_act_table_set(LOG_EXP)
            e.wait_ge(s_ld[0], 64)
            e.activation(a_neg[:, :, :], a_neg[:, :, :], ACT.Exp).then_inc(s_ca, 1)
            e.wait_ge(s_ca, 1)
            e.activation(a_neg[:, :, :], a_neg[:, :, :], ACT.Copy, scale=-1.0).then_inc(s_ca, 1)
            e.wait_ge(s_ca, 2)
            e.wait_ge(s_c, KD + ND * TAPS + 3)
            e.wait_ge(s_id, 13)

            def front(c):
                scales.wait(e, c)
                if not (isinstance(c, int) and c == 0):
                    for t in range(NT // 2):
                        wait_read(e, "M", c - 1, t)
                for b in range(NT):
                    xres_ok.by(e.activation(xres[:, b, :], xin[:, b, :], ACT.Identity,
                                            bias=st[:, 9, b:b + 1], scale=st[:, 10, b:b + 1]))
                xres_ok.wait(e, c)
                for b in range(NT):
                    xn_ok.by(e.activation(xin[:, b, :], xin[:, b, :], ACT.Identity,
                                          bias=st[:, 8, b:b + 1], scale=st[:, 6, b:b + 1]))
                for k in range(KD):
                    bank = wait_full(e, "F", c, F_XT + k)
                    read_out(e.activation(xT[:, k, :], bank[:, :], ACT.Copy), F_XT + k)
                dt_ok.wait(e, c - 1)
                for d in range(ND):
                    bank = wait_full(e, "F", c, F_IN + d)
                    read_out(e.activation(xpre[:, d, HALO:HALO + TC], bank[:, :], ACT.Copy), F_IN + d)
                e.preload_act_table(ACT.Silu)
                yg_ok.wait(e, c - 1)
                for d in range(ND):
                    bank = wait_full(e, "F", c, F_IN + ND + d)
                    read_out(e.activation(sres[:, d, :], bank[:, :], ACT.Silu), F_IN + ND + d)
                u_ok.wait(e, c - 1)
                for d in range(ND):
                    bank = wait_full(e, "F", c, F_CONV + d)
                    read_out(e.activation(xs[:, d, :], bank[:, :], ACT.Silu, bias=cb[:, d:d + 1]), F_CONV + d)
                halo_ok.by(e.activation(xpre[:, :, 0:HALO], xpre[:, :, TC:TC + HALO], ACT.Copy))
                e.preload_act_table_set(LOG_EXP)
                halo_ok.wait(e, c)
                for d in range(ND):
                    bank = wait_full(e, "F", c, F_DT + d)
                    soft.by(e.activation(xpre[:, d, HALO:HALO + TC], bank[:, :], ACT.Relu))
                    read_out(e.activation(hb[:, d, :], bank[:, :], ACT.Abs), F_DT + d)
                    wait_read(e, "F", c, F_DT + d)
                    soft.by(e.activation(hb[:, d, :], hb[:, d, :], ACT.Exp, scale=-1.0))
                    soft.wait(e, c, 3 * d + 2)
                    soft.by(e.activation(hb[:, d, :], hb[:, d, :], ACT.Ln, bias=1.0))
                ch_ok.wait(e, c - 1)
                for k in range(2 * N):
                    if k % (2 * NG) >= NG:
                        n = k // (2 * NG) * NG + k % NG
                        bank = wait_full(e, "F", c, F_SPREAD + k)
                        read_out(e.activation(c_all[:, n, :], bank[:, :], ACT.Copy), F_SPREAD + k)

            def decays(c, q):
                d = q // GPD
                dt_ok.wait(e, c, d + 1)
                for n in range(NG):
                    j = q * NG + n
                    h_ok.wait(e, c, j - 1)
                    s = (q % GPD) * NG + n
                    e_ok.by(e.activation(ebank[j % 2][:, :], dt_[:, d, :], ACT.Exp, scale=a_neg[:, d, s:s + 1]))

            def normal(c):
                scales2.wait(e, c)
                wait_full(e, "O", c - 1, O_XT + KD - 1) if not (isinstance(c, int) and c == 0) else None
                for b in range(NT):
                    xn2_ok.by(e.activation(xn2[:, b, :], x1[:, b, :], ACT.Identity,
                                           bias=st2[:, 3, b:b + 1], scale=st2[:, 1, b:b + 1]))

            def turned(c):
                for k in range(KD):
                    bank = wait_full(e, "O", c, O_XT + k)
                    read_out(e.activation(xT[:, k, :], bank[:, :], ACT.Copy), O_XT + k)

            def gate(c, f):
                bank = wait_full(e, "O", c, O_GATE + f)
                read_out(e.activation(hb[:, f, :], bank[:, :], ACT.Copy), O_GATE + f)

            def silus(c):
                bank = wait_full(e, "O", c, O_TAIL)
                silu_ok.by(e.activation(hb[FR:P, FT, :], bank[0:FR, :], ACT.Copy))
                e.preload_act_table(ACT.Silu)
                wait_read(e, "O", c, O_GATE + FT - 1)
                silu_ok.by(e.activation(hb[:, 0:FT, :], hb[:, 0:FT, :], ACT.Silu))
                silu_ok.wait(e, c, 1)
                silu_ok.by(e.activation(hb[FR:P, FT, :], hb[FR:P, FT, :], ACT.Silu))
                e.preload_act_table_set(LOG_EXP)

            BACK = {1: (normal,), 2: (turned,), 3: (lambda c: gate(c, 0),), 4: (lambda c: gate(c, 1),), 5: (lambda c: gate(c, 2),),
                    6: (lambda c: gate(c, 3),), 7: (lambda c: gate(c, 4),), 8: (silus,)}

            def iteration(i, with_back):
                front(i)
                for q in range(Q):
                    decays(i, q)
                    if with_back:
                        if q == 3:
                            dt_ok.wait(e, i)
                        for job in BACK.get(q, ()):
                            job(i - 1)

            iteration(0, False)
            with e.Fori(1, E) as i:
                iteration(i, True)
            for q in range(Q):
                for job in BACK.get(q, ()):
                    job(E - 1)

        @block.tensor
        def _(e):
            def product(out_ap, terms):
                for n, (a, b) in enumerate(terms):
                    last = e.matmul(out_ap, a, b, start=(n == 0), stop=(n == len(terms) - 1))
                return last

            def cols(n):
                return slice(n * P, (n + 1) * P)

            e.wait_ge(s_id, 13)
            e.wait_ge(s_ld[1], 16)
            for j in range(ND):
                for k in range(ND):
                    last = e.transpose(gbank[j][:, cols(k)], wx_ld[:, k, cols(j)], ident[:, :])
                last.then_inc(s_tr, 1)
            e.wait_ge(s_ld[2], 16)
            e.wait_ge(s_tc, ND)
            for k in range(ND):
                product(gbank[k][:, :], [(wxT[:, j, cols(k)], wdt_ld[:, j, :]) for j in range(ND)]).then_inc(s_tr, 1)
            e.wait_ge(s_tc, 2 * ND)
            e.wait_ge(s_c, KD + ND * TAPS + 3)
            e.wait_ge(s_ca, 2)

            def transposes(c, stage, first, src, done):
                done.wait(e, c)
                for k in range(KD):
                    bank = wait_free(e, stage, c, first + k)
                    for b in range(NT):
                        last = e.transpose(bank[:, cols(b)], src[:, b, cols(k)], ident[:, :])
                    filled(last, first + k)

            def front(c):
                transposes(c, "F", F_XT, xin, xn_ok)
                for k in range(KD):
                    wait_read(e, "F", c, F_XT + k)
                for m in range(2 * ND):
                    bank = wait_free(e, "F", c, F_IN + m)
                    filled(product(bank[:, :], [(win[:, k, cols(m)], xT[:, k, :]) for k in range(KD)]), F_IN + m)
                for d in range(ND):
                    bank = wait_free(e, "F", c, F_CONV + d)
                    filled(product(bank[:, :], [(cdiag[:, d, k, :], xpre[:, d, k:k + TC]) for k in range(TAPS)]), F_CONV + d)
                for d in range(ND):
                    wait_read(e, "F", c, F_CONV + d)
                for d in range(ND):
                    bank = wait_free(e, "F", c, F_DT + d)
                    filled(product(bank[:, :], [(wc[:, k, cols(d)], xs[:, k, :]) for k in range(ND)]), F_DT + d)
                bank = wait_free(e, "F", c, F_BC)
                filled(product(bank[0:6 * N, :], [(wbc[:, k, :, :].rearrange("p r n -> p (r n)"), xs[:, k, :]) for k in range(ND)]), F_BC)
                bc_ok.wait(e, c)
                for k in range(2 * N):
                    n = k // (2 * NG) * NG + k % NG + (N if k % (2 * NG) >= NG else 0)
                    bank = wait_free(e, "F", c, F_SPREAD + k)
                    filled(e.matmul(bank[:, :], pick[:, n:n + 1].broadcast_to([6 * N, P]), bc_s[:, :], start=True, stop=True), F_SPREAD + k)

            def add_up(c, q):
                if q % GPD == 0:
                    yg_ok.wait(e, c, q // GPD)
                ch_ok.wait(e, c, q + 1)
                for n in range(NG):
                    last = e.matmul(ybank[:, :], ident[:, :], ring[:, q % RING, n, :],
                                    start=(q % GPD == 0 and n == 0), stop=(q % GPD == GPD - 1 and n == NG - 1))
                y_ok.by(last)

            def turn(c):
                transposes(c, "O", O_XT, xn2, xn2_ok)

            def expand(c, j, f, use):
                if use == O_GATE:
                    w13_in.wait(e, c)
                    for k in range(KD):
                        wait_read(e, "O", c, O_XT + k)
                bank = wait_free(e, "O", c, use)
                filled(product(bank[:, :], [(w13[:, k, j, cols(f)], xT[:, k, :]) for k in range(KD)]), use)

            def tail(c):
                bank = wait_free(e, "O", c, O_TAIL)
                filled(product(bank[:, :], [(w13t[:, k, :], xT[:, k, :]) for k in range(KD)]), O_TAIL)

            def contract(c, t):
                w2_in.wait(e, c)
                for k in range(O_UP + FT - NB, O_UP + FT):
                    wait_read(e, "O", c, k)
                bank = wait_free(e, "O", c, O_DOWN + t)
                for b in range(2):
                    tok = cols(2 * t + b)
                    last = product(bank[:, b * D:(b + 1) * D], [(hb[:, f, tok], w2s[:, f, :]) for f in range(FT)]
                                   + [(hb[FR:P, FT, tok], w2s[FR:P, FT, :])])
                filled(last, O_DOWN + t)

            def project(c):
                yg_ok.wait(e, c)
                for t in range(NT // 2):
                    bank = wait_free(e, "M", c, t)
                    for b in range(2):
                        last = product(bank[:, b * D:(b + 1) * D], [(sres[:, k, cols(2 * t + b)], wout[:, k, :]) for k in range(ND)])
                    filled(last, t)

            BACK = {1: (turn,), 7: (tail,), 13: (lambda c: contract(c, 0),), 14: (lambda c: contract(c, 1),)}
            for f in range(FT):
                BACK[2 + f] = (lambda c, f=f: expand(c, 0, f, O_GATE + f),)
                BACK[8 + f] = (lambda c, f=f: expand(c, 1, f, O_UP + f),)

            def iteration(i, with_back):
                front(i)
                for q in range(Q):
                    add_up(i, q)
                    if with_back:
                        for job in BACK.get(q, ()):
                            job(i - 1)
                project(i)

            iteration(0, False)
            with e.Fori(1, E) as i:
                iteration(i, True)
            for q in range(Q):
                for job in BACK.get(q, ()):
                    job(E - 1)


_INS = ["L0_attn_x", "L0_attn_rms_w", "L0_attn_W_in", "L0_attn_conv_w", "L0_attn_conv_b", "L0_attn_W_x", "L0_attn_W_dt",
        "L0_attn_A_log", "L0_attn_W_out", "L0_ffn_w1", "L0_ffn_w3", "L0_ffn_w2"]


def kernel(**inputs):
    import numpy as _np
    import concourse.bacc as _bacc
    from concourse import mybir as _mybir
    from concourse.bass_utils import run_bass_kernel_spmd as _run

    nc = _bacc.Bacc("TRN2", target_bir_lowering=False, num_devices=1)
    arrays, args = {}, []
    for name in _INS:
        a = _np.ascontiguousarray(inputs[name])
        arrays[f"in_{name}_dram"] = a
        args.append(nc.dram_tensor(f"in_{name}_dram", a.shape, _mybir.dt.from_np(a.dtype), kind="ExternalInput").ap())
    shape = inputs["L0_attn_x"].shape
    args.append(nc.dram_tensor("out_dram", shape, f32, kind="ExternalOutput").ap())
    mamba_moe_layer(nc, *args)
    r = _run(nc, [arrays], core_ids=[0])
    return r.results[0]["out_dram"]
```

```python
import concourse.bass as bass
from concourse import mybir
from contextlib import ExitStack

f32 = mybir.dt.float32
bf16 = mybir.dt.bfloat16
ALU = mybir.AluOpType
ACT = mybir.ActivationFunctionType


def mamba_moe_layer(nc, x, rms_w, W_in, conv_w, conv_b, W_x, W_dt, A_log, W_out, w1, w3, w2, out):
    T, D = x.shape[1], x.shape[2]
    DI, N = A_log.shape
    TAPS = conv_w.shape[2]
    E, _, FF = w1.shape
    P = 128
    TC = T // E
    NT = TC // P
    KD = D // P
    ND = DI // P
    HALO = TAPS - 1
    NG = 2
    GPD = N // NG
    Q = ND * GPD
    NS = Q * NG
    RING = 4
    SG = 4
    FT = FF // P
    FR = FF - FT * P
    W = 2 * N
    assert FR * 2 == P and Q % RING == 0 and TC == 512 and 3 * W <= P
    EPS = 1e-5

    ctx = ExitStack()
    with ctx:
        def sb(name, shape, dt=f32):
            return ctx.enter_context(nc.sbuf_tensor(name, shape, dt))

        def pb(name):
            return ctx.enter_context(nc.psum_tensor(name, [P, TC], f32))

        def sem(name):
            return ctx.enter_context(nc.semaphore(name))

        b_all = sb("b_all", [P, N, TC])
        c_all = sb("c_all", [P, N, TC])
        ring = sb("ring", [P, RING, NG, TC])
        dt_ = sb("dt_", [P, ND, TC])
        xs = sb("xs", [P, ND, TC])
        u_kept = sb("u_kept", [P, ND - 2, TC])
        sres_n = sb("sres_n", [P, ND, TC])
        sres = sb("sres", [P, ND, TC])
        xin = sb("xin", [P, NT, D])
        xT = sb("xT", [P, KD, TC])
        xpre = sb("xpre", [P, ND, HALO + TC])
        hb = sb("hb", [P, FT + 1, TC])
        up_t = sb("up_t", [P, TC])
        x1 = sb("x1", [P, NT, D])
        xn2 = sb("xn2", [P, NT, D])
        bc_r = sb("bc_r", [3 * W, TC])
        bc_s = sb("bc_s", [3 * W, TC], bf16)
        win = sb("win", [P, KD, 2 * DI])
        wc = sb("wc", [P, ND, DI])
        wbc = sb("wbc", [P, ND, 3, W])
        wout = sb("wout", [P, ND, D])
        cdiag = sb("cdiag", [P, ND, TAPS, P])
        w13 = sb("w13", [P, KD, 2, FT * P])
        w13t = sb("w13t", [P, KD, P])
        w2s = sb("w2s", [P, FT + 1, D])
        ident = sb("ident", [P, P])
        pick = sb("pick", [3 * W, W], bf16)
        a_neg = sb("a_neg", [P, ND, N])
        cw = sb("cw", [P, ND, TAPS])
        cb = sb("cb", [P, ND])
        rw = sb("rw", [P, KD])
        state = sb("state", [P, Q, NG])
        bn = sb("bn", [P, NT, 6])
        mv = sb("mv", [P, NT, 2])
        bn2 = sb("bn2", [P, NT, 6])
        mv2 = sb("mv2", [P, NT, 2])
        st = sb("st", [P, 11, NT])
        kept = sb("kept", [P, 2, 2, NT])
        st2 = sb("st2", [P, 4, NT])
        consts = sb("consts", [P, 6, NT])
        taken = sb("taken", [1, 1])
        wx_ld = hb[:, :, :].rearrange("p a b -> p (a b)")[:, 0:ND * (DI + W)].rearrange("p (k n) -> p k n", k=ND)
        wxT = ring[:, :, :, :].rearrange("p r g t -> p (r g) t")[:, 0:ND, :]
        wdt_ld = ring[:, :, :, :].rearrange("p r g t -> p (r g) t")[:, ND:2 * ND, :]

        ubank = pb("ubank")
        ybank = pb("ybank")
        ebank = [pb("ebank0"), pb("ebank1")]
        gbank = [pb(f"gbank{b}") for b in range(4)]
        NB = len(gbank)

        USES = [(name, k) for name, ks in (
            ("M", range(NT // 2)), ("XT", range(KD)), ("IN", range(ND)), ("RES", range(ND)), ("CV", range(ND // 2)),
            ("OXT", range(KD)), ("CV", range(ND // 2, ND)), ("GATE", range(FT)), ("TAIL", range(1)), ("BC", range(1)),
            ("DT", range(ND)), ("UP", range(FT)), ("DOWN", range(NT // 2)), ("SP", range(2 * N))) for k in ks]
        assert len(USES) % NB == 0
        PER = len(USES) // NB
        POS = {use: p for p, use in enumerate(USES)}
        OF_BACK = ("M", "OXT", "GATE", "TAIL", "UP", "DOWN")
        full = [sem(f"full{b}") for b in range(NB)]
        free = [sem(f"free{b}") for b in range(NB)]

        def known(i):
            return isinstance(i, int)

        def has_front(i):
            return not known(i) or i < E - 1

        def has_scan(i):
            return not known(i) or 0 <= i < E

        def has_back(i):
            return not known(i) or i >= 1

        def there(use, i):
            return has_back(i) if use[0] in OF_BACK else has_front(i)

        def uses_of(b, i, before=len(USES)):
            return sum(there(USES[p], i) for p in range(b, before, NB))

        lacking = [2 * PER - uses_of(b, -1) - uses_of(b, 0) for b in range(NB)]

        def nth(i, name, k):
            p = POS[name, k]
            b = p % NB
            if known(i):
                return b, lacking[b] + sum(uses_of(b, j) for j in range(-1, i)) + uses_of(b, i, p) + 1
            return b, (i + 1) * PER + p // NB + 1

        def wait_full(e, i, name, k):
            b, n = nth(i, name, k)
            e.wait_ge(full[b], n)
            return gbank[b]

        def wait_read(e, i, name, k):
            b, n = nth(i, name, k)
            e.wait_ge(free[b], n)

        def wait_free(e, i, name, k):
            b, n = nth(i, name, k)
            e.wait_ge(free[b], n - 1)
            return gbank[b]

        def filled(ins, name, k):
            ins.then_inc(full[POS[name, k] % NB], 1)

        def read_out(ins, name, k):
            ins.then_inc(free[POS[name, k] % NB], 1)

        events = []

        class Event:
            def __init__(self, name, number):
                self.sem, self.number = sem("s_" + name), number
                events.append(self)

            def wait(self, e, c, j=None):
                n = (c + 1) * self.number + (self.number if j is None else j)
                if not known(n) or n > self.number:
                    e.wait_ge(self.sem, n)

            def by(self, ins):
                ins.then_inc(self.sem, 1)

        x_in, x1_in, w13_in, w2_in, stored = (Event(n, k) for n, k in (
            ("x_in", 16), ("x1_in", 16), ("w13_in", 64), ("w2_in", 32), ("stored", 16)))
        bn_ok = Event("bn_ok", 1)
        stats = Event("stats", 1)
        scales = Event("scales", 11)
        kept_ok = Event("kept_ok", 2)
        xn_ok = Event("xn_ok", NT)
        halo_ok = Event("halo_ok", 1)
        xs_ok = Event("xs_ok", 2)
        soft = Event("soft", 3 * ND)
        dt_ok = Event("dt_ok", ND)
        bc_ok = Event("bc_ok", 4)
        u_ok = Event("u_ok", ND)
        uk_ok = Event("uk_ok", ND - 2)
        sr_ok = Event("sr_ok", 1)
        bu_ok = Event("bu_ok", Q)
        e_ok = Event("e_ok", NS)
        h_ok = Event("h_ok", NS)
        st_ok = Event("st_ok", Q)
        ch_ok = Event("ch_ok", 2 * Q)
        y_ok = Event("y_ok", Q)
        yg_ok = Event("yg_ok", ND)
        x1a_ok = Event("x1a_ok", NT)
        bn2_ok = Event("bn2_ok", 1)
        stats2 = Event("stats2", 1)
        scales2 = Event("scales2", 4)
        xn2_ok = Event("xn2_ok", NT)
        silu_ok = Event("silu_ok", 3)
        tail_ok = Event("tail_ok", 1)

        s_ld = [sem(f"s_ld{n}") for n in range(4)]
        s_id = sem("s_id")
        s_c = sem("s_c")
        s_ca = sem("s_ca")
        s_tr = sem("s_tr")
        s_tc = sem("s_tc")
        POOL_CONSTS, DVE_CONSTS = 17, KD + ND * TAPS + 3

        block = ctx.enter_context(nc.Block())

        def rows(t, c):
            return t[0, bass.ds(c * TC, TC), :].rearrange("(b p) d -> p b d", p=P)

        def run(e, table, group=None, before=None, after=None):
            def iteration(i):
                on = {"front": (has_front(i), i + 1), "scan": (has_scan(i), i), "back": (has_back(i), i - 1)}
                if has_scan(i) and before:
                    before(i)
                for q in range(Q):
                    if has_scan(i) and group:
                        group(i, q)
                    for at, part, job in table:
                        if at == q and on[part][0]:
                            job(on[part][1], i)
                if after:
                    after(i)

            iteration(-1)
            iteration(0)
            with e.Fori(1, E - 1) as i:
                iteration(i)
            iteration(E - 1)
            iteration(E)

        @block.sync
        def _(e):
            for ev in events:
                e.sem_inc(ev.sem, ev.number)
            for b in range(NB):
                e.sem_inc(full[b], lacking[b])
                e.sem_inc(free[b], lacking[b])

            def load_x(c):
                e.dma_start(xin[:, :, :], rows(x, c)).then_inc(x_in.sem, 16)

            def load_x1(c):
                e.dma_start(x1[:, :, :], rows(x, c)).then_inc(x1_in.sem, 16)

            def load_w13(c):
                for j, w in enumerate((w1, w3)):
                    src = w[bass.ds(c, 1), :, :].rearrange("a (k p) f -> p (a k) f", p=P)
                    e.dma_start(w13[:, :, j, :], src[:, :, 0:FT * P]).then_inc(w13_in.sem, 16)
                    e.dma_start(w13t[:, :, j * FR:(j + 1) * FR], src[:, :, FT * P:FF]).then_inc(w13_in.sem, 16)

            def load_w2(c):
                e.dma_start(w2s[:, 0:FT, :], w2[bass.ds(c, 1), 0:FT * P, :].rearrange("a (k p) d -> p (a k) d", p=P)).then_inc(w2_in.sem, 16)
                e.dma_start(w2s[P - FR:P, FT:FT + 1, :], w2[bass.ds(c, 1), FT * P:FF, :].rearrange("a p d -> p a d")).then_inc(w2_in.sem, 16)

            load_x(0)
            e.dma_start(cw[:, :, :], conv_w.rearrange("(d p) a k -> p d (a k)", p=P)).then_inc(s_ld[0], 16)
            e.dma_start(cb[:, :], conv_b.rearrange("(d p) -> p d", p=P), allow_slow_non_contiguous=True).then_inc(s_ld[0], 16)
            e.dma_start(rw[:, :], rms_w.rearrange("(d p) -> p d", p=P), allow_slow_non_contiguous=True).then_inc(s_ld[0], 16)
            e.dma_start(a_neg[:, :, :], A_log.rearrange("(d p) n -> p d n", p=P)).then_inc(s_ld[0], 16)
            e.dma_start(wx_ld, W_x.rearrange("(k p) n -> p k n", p=P)).then_inc(s_ld[1], 16)
            e.dma_start(win[:, :, :], W_in.rearrange("(k p) n -> p k n", p=P)).then_inc(s_ld[3], 16)
            e.dma_start(wdt_ld, W_dt.rearrange("(k p) n -> p k n", p=P)).then_inc(s_ld[2], 16)
            e.dma_start(wout[:, :, :], W_out.rearrange("(k p) n -> p k n", p=P)).then_inc(s_ld[3], 16)
            load_x1(0)
            load_w13(0)
            load_w2(0)

            def next_x(i):
                xs_ok.wait(e, i, 1)
                load_x(i + 1)

            def back(i):
                if not known(i) or i < E:
                    wait_full(e, i, "UP", FT - 1)
                    load_w13(i)
                    for t in range(NT // 2):
                        wait_full(e, i, "DOWN", t)
                    load_w2(i)
                for t in range(NT // 2):
                    wait_read(e, i, "DOWN", t)
                e.dma_start(rows(out, i - 1), x1[:, :, :]).then_inc(stored.sem, 16)
                stored.wait(e, i - 1)
                if not known(i) or i < E:
                    load_x1(i)

            next_x(0)
            with e.Fori(1, E - 1) as i:
                next_x(i)
                back(i)
            back(E - 1)
            back(E)

        @block.gpsimd
        def _(e):
            made = [0]

            def step(ins):
                made[0] += 1
                ins.then_inc(s_id, 1)
                e.wait_ge(s_id, made[0])

            step(e.memset(ident[:, :], 0.0))
            step(e.affine_select(out=ident[:, :], in_=ident[:, :], compare_op=ALU.not_equal, fill=1.0,
                                 base=0, pattern=[[-1, P]], channel_multiplier=1))
            for n, value in enumerate((-0.5, EPS, -1.0, 1.0, 0.0, 0.0)):
                step(e.memset(consts[:, n, :], value))
            step(e.memset(pick[:, :], 0.0))
            step(e.memset(state[:, :, :], 0.0))
            step(e.memset(xpre[:, :, 0:HALO], 0.0))
            step(e.memset(st[:, :, :], 0.0))
            step(e.memset(kept[:, :, :, :], 0.0))
            for r in range(3):
                step(e.affine_select(out=pick[:, :], in_=pick[:, :], compare_op=ALU.not_equal, fill=1.0,
                                     base=-r * W, pattern=[[-1, W]], channel_multiplier=1))
            step(e.memset(taken[:, :], 0.0))
            assert made[0] == POOL_CONSTS
            mhalf, eps, minus, one, zero = (consts[:, n, :] for n in range(5))
            zeros = consts[:, 4:6, :]

            def hand_on(c, i):
                if has_scan(i):
                    scales.wait(e, i)
                x1a_ok.wait(e, i - 2)
                kept_ok.by(e.tensor_tensor(kept[:, 1, :, :], kept[:, 0, :, :], zeros, ALU.add))
                kept_ok.wait(e, i, 1)
                if has_scan(i):
                    kept_ok.by(e.tensor_tensor(kept[:, 0, :, :], st[:, 9:11, :], zeros, ALU.add))

            def front(c, i):
                j = [0]

                def then(ins):
                    j[0] += 1
                    scales.by(ins)
                    scales.wait(e, c, j[0])

                m, v = mv[:, :, 0], mv[:, :, 1]
                ve, r, vr, ms, mse, r2, s, nm, bs, br, rp = (st[:, n, :] for n in range(11))
                stats.wait(e, c)
                xn_ok.wait(e, c - 1)
                if not known(i) or i != -1:
                    kept_ok.wait(e, i)
                then(e.tensor_tensor(ve, v, eps, ALU.add))
                then(e.tensor_tensor(r, ve, mhalf, ALU.pow))
                then(e.tensor_tensor(vr, v, r, ALU.mult))
                then(e.tensor_tensor(ms, vr, r, ALU.mult))
                then(e.tensor_tensor(mse, ms, eps, ALU.add))
                then(e.tensor_tensor(r2, mse, mhalf, ALU.pow))
                then(e.tensor_tensor(s, r, r2, ALU.mult))
                then(e.tensor_tensor(nm, m, minus, ALU.mult))
                then(e.tensor_tensor(bs, nm, s, ALU.mult))
                then(e.tensor_tensor(br, nm, r, ALU.mult))
                then(e.tensor_tensor(rp, r, one, ALU.add))

            def group(c, q):
                slot, n = ring[:, q % RING, :, :], q % GPD * NG
                h_ok.wait(e, c, NG * (q + 1))
                st_ok.by(e.tensor_tensor(state[:, q, :], slot[:, :, TC - 1], zero[:, 0:NG], ALU.add))
                st_ok.wait(e, c, q + 1)
                if q < GPD:
                    for k in range(n, n + NG):
                        wait_read(e, c - 1, "SP", k // SG * 2 * SG + SG + k % SG)
                ch_ok.by(e.tensor_tensor(slot, slot, c_all[:, n:n + NG, :], ALU.mult))
                ch_ok.wait(e, c, 2 * q + 1)
                ch_ok.by(e.tensor_tensor(slot[:, 0, :], slot[:, 0, :], slot[:, 1, :], ALU.add))

            def back(c, i):
                def then(ins, j):
                    scales2.by(ins)
                    scales2.wait(e, c, j)

                stats2.wait(e, c)
                xn2_ok.wait(e, c - 1)
                then(e.tensor_tensor(st2[:, 0, :], mv2[:, :, 1], eps, ALU.add), 1)
                then(e.tensor_tensor(st2[:, 1, :], st2[:, 0, :], mhalf, ALU.pow), 2)
                then(e.tensor_tensor(st2[:, 2, :], mv2[:, :, 0], minus, ALU.mult), 3)
                then(e.tensor_tensor(st2[:, 3, :], st2[:, 2, :], st2[:, 1, :], ALU.mult), 4)

            table = [(0, "scan", hand_on), (0, "back", lambda c, i: hand_on(c, i) if not has_scan(i) else None),
                     (0, "front", front), (7, "back", back)]
            run(e, table, group)

        @block.vector
        def _(e):
            e.wait_ge(s_ld[1], 16)
            for r in range(3):
                e.tensor_copy(wbc[:, :, r, :], wx_ld[:, :, DI:DI + W]).then_inc(s_c, 1)
            for j in range(ND):
                e.wait_ge(s_tr, j + 1)
                e.tensor_copy(wxT[:, j, :], gbank[j][:, :]).then_inc(s_tc, 1)
            e.wait_ge(s_ld[0], 64)
            e.wait_ge(s_ld[3], 32)
            for k in range(KD):
                e.tensor_scalar(win[:, k, :], win[:, k, :], rw[:, k:k + 1], None, ALU.mult).then_inc(s_c, 1)
            e.wait_ge(s_id, POOL_CONSTS)
            for d in range(ND):
                for k in range(TAPS):
                    e.tensor_scalar(cdiag[:, d, k, :], ident[:, :], cw[:, d, k:k + 1], None, ALU.mult).then_inc(s_c, 1)
            for k in range(ND):
                e.wait_ge(s_tr, ND + k + 1)
                e.tensor_copy(wc[:, k, :], gbank[k][:, :]).then_inc(s_tc, 1)

            def take():
                e.tensor_copy(taken[:, :], rw[0:1, 0:1])

            def row_stats(c, src, tmp, dst, first, second):
                for b in range(NT):
                    last = e.bn_stats(tmp[:, b, :], src[:, b, :])
                first.by(last)
                first.wait(e, c)
                take()
                for b in range(NT):
                    last = e.bn_aggr(dst[:, b, :], tmp[:, b, :])
                second.by(last)

            def x_stats(c, i):
                x_in.wait(e, c)
                stats.wait(e, c - 1)
                scales.wait(e, c - 1)
                row_stats(c, xin, bn, mv, bn_ok, stats)

            def split_bc(c, i):
                bank = wait_full(e, i, "BC", 0)
                bc_ok.wait(e, c - 1)
                bc_ok.by(e.tensor_copy(bc_s[:, :], bank[0:3 * W, :]))
                bc_ok.wait(e, c, 1)
                read_out(e.tensor_tensor(bc_r[:, :], bank[0:3 * W, :], bc_s[:, :], ALU.subtract), "BC", 0)
                wait_read(e, i, "BC", 0)
                for r in (1, 2):
                    bc_ok.by(e.tensor_copy(bc_s[r * W:(r + 1) * W, :], bc_r[r * W:(r + 1) * W, :]))
                bc_ok.wait(e, c, 3)
                third = slice(2 * W, 3 * W)
                bc_ok.by(e.tensor_tensor(bc_s[third, :], bc_r[third, :], bc_s[third, :], ALU.subtract))

            def dt_of(d):
                def job(c, i):
                    soft.wait(e, c, 3 * (d + 1))
                    dt_ok.by(e.scalar_tensor_tensor(dt_[:, d, :], xpre[:, d, HALO:HALO + TC], 0.0, dt_[:, d, :], ALU.max, ALU.add))
                return job

            def keep_u(c, i):
                dt_ok.wait(e, c)
                u_ok.wait(e, c - 1)
                for d in range(2, ND):
                    uk_ok.by(e.tensor_tensor(u_kept[:, d - 2, :], dt_[:, d, :], xs[:, d, :], ALU.mult))

            def u_of(c, d):
                bu_ok.wait(e, c, d * GPD)
                if d < 2:
                    dt_ok.wait(e, c, d + 1)
                    xs_ok.wait(e, c, 1)
                    u_ok.by(e.tensor_tensor(ubank[:, :], dt_[:, d, :], xs[:, d, :], ALU.mult))
                else:
                    uk_ok.wait(e, c, d - 1)
                    u_ok.by(e.tensor_copy(ubank[:, :], u_kept[:, d - 2, :]))

            def bu(c, q):
                n = q % GPD * NG
                u_ok.wait(e, c, q // GPD + 1)
                y_ok.wait(e, c, q - RING + 1)
                if q < GPD:
                    for k in range(n, n + NG):
                        wait_read(e, c - 1, "SP", k // SG * 2 * SG + k % SG)
                bu_ok.by(e.tensor_tensor(ring[:, q % RING, :, :], b_all[:, n:n + NG, :],
                                         ubank[:, :].unsqueeze(1).broadcast_to([P, NG, TC]), ALU.mult))

            def start(c):
                u_of(c, 0)
                bu(c, 0)

            def group(c, q):
                bu_ok.wait(e, c, q + 1)
                st_ok.wait(e, c - 1, q + 1)
                for n in range(NG):
                    j = q * NG + n
                    e_ok.wait(e, c, j + 1)
                    row = ring[:, q % RING, n, :]
                    h_ok.by(e.tensor_tensor_scan(row, ebank[j % 2][:, :], row, initial=state[:, q, n:n + 1],
                                                 op0=ALU.mult, op1=ALU.add))
                if q + 1 < Q:
                    if (q + 1) % GPD == 0:
                        u_of(c, (q + 1) // GPD)
                    bu(c, q + 1)

            def gated(d):
                def job(c, i):
                    y_ok.wait(e, c, GPD * (d + 1))
                    sr_ok.wait(e, c)
                    yg_ok.by(e.tensor_tensor(sres[:, d, :], ybank[:, :], sres[:, d, :], ALU.mult))
                return job

            def add_rows(name, t, ready):
                def job(c, i):
                    bank = wait_full(e, i, name, t)
                    ready.wait(e, c)
                    two = x1[:, 2 * t:2 * t + 2, :]
                    read_out(e.tensor_tensor(two, two, bank[:, :].rearrange("p (b d) -> p b d", b=2), ALU.add), name, t)
                return job

            def x1_stats(c, i):
                for t in range(NT // 2):
                    wait_read(e, i, "M", t)
                stats2.wait(e, c - 1)
                scales2.wait(e, c - 1)
                row_stats(c, x1, bn2, mv2, bn2_ok, stats2)

            def hidden(f):
                def job(c, i):
                    silu_ok.wait(e, c, 2)
                    bank = wait_full(e, i, "UP", f)
                    read_out(e.tensor_tensor(hb[:, f, :], hb[:, f, :], bank[:, :], ALU.mult), "UP", f)
                return job

            def hidden_tail(c, i):
                silu_ok.wait(e, c, 3)
                wait_read(e, i, "TAIL", 0)
                tail_ok.by(e.tensor_tensor(hb[FR:P, FT, :], hb[FR:P, FT, :], up_t[FR:P, :], ALU.mult))

            table = [(0, "front", x_stats), (2, "back", gated(ND - 1)), (4, "scan", dt_of(ND - 1)), (5, "scan", keep_u),
                     (5, "back", add_rows("M", 0, x1a_ok)), (6, "back", add_rows("M", 1, x1a_ok)), (6, "back", x1_stats),
                     (17, "front", split_bc), (19, "front", dt_of(0)), (20, "front", dt_of(1)),
                     (22, "back", hidden_tail), (22, "back", hidden(0)), (22, "back", hidden(1)),
                     (23, "back", hidden(2)), (23, "back", hidden(3)), (24, "back", hidden(4)),
                     (26, "front", dt_of(2)), (26, "back", add_rows("DOWN", 0, xn2_ok)), (28, "back", add_rows("DOWN", 1, xn2_ok))]
            table += [(GPD * (d + 1) + 2, "scan", gated(d)) for d in range(ND - 1)]
            run(e, table, group, before=start)

        @block.scalar
        def _(e):
            LOG_EXP = "natural_log_exp_and_others"
            e.preload_act_table_set(LOG_EXP)
            e.wait_ge(s_ld[0], 64)
            e.activation(a_neg[:, :, :], a_neg[:, :, :], ACT.Exp).then_inc(s_ca, 1)
            e.wait_ge(s_ca, 1)
            e.activation(a_neg[:, :, :], a_neg[:, :, :], ACT.Copy, scale=-1.0).then_inc(s_ca, 1)
            e.wait_ge(s_ca, 2)
            e.wait_ge(s_c, DVE_CONSTS)
            e.wait_ge(s_id, POOL_CONSTS)

            def group(c, q):
                d = q // GPD
                dt_ok.wait(e, c, d + 1)
                for n in range(NG):
                    j = q * NG + n
                    h_ok.wait(e, c, j - 1)
                    k = q % GPD * NG + n
                    e_ok.by(e.activation(ebank[j % 2][:, :], dt_[:, d, :], ACT.Exp, scale=a_neg[:, d, k:k + 1]))

            def move(name, k, i, dst, bias=None):
                bank = wait_full(e, i, name, k)
                if bias is None:
                    ins = e.activation(dst, bank[:, :], ACT.Copy)
                else:
                    ins = e.activation(dst, bank[:, :], ACT.Identity, bias=bias)
                read_out(ins, name, k)

            def normal(c, i):
                scales.wait(e, c)
                for b in range(NT):
                    xn_ok.by(e.activation(xin[:, b, :], xin[:, b, :], ACT.Identity,
                                          bias=st[:, 8, b:b + 1], scale=st[:, 6, b:b + 1]))

            def turned(name):
                def job(c, i):
                    for k in range(KD):
                        move(name, k, i, xT[:, k, :])
                return job

            def before_conv(*ds):
                def job(c, i):
                    for d in ds:
                        dt_ok.wait(e, c - 1, d + 1)
                        move("IN", d, i, xpre[:, d, HALO:HALO + TC])
                return job

            def res(*ds):
                def job(c, i):
                    sr_ok.wait(e, c - 1)
                    for d in ds:
                        move("RES", d, i, sres_n[:, d, :])
                return job

            def convolved(*ds):
                def job(c, i):
                    for d in ds:
                        if d < 2:
                            u_ok.wait(e, c - 1, d + 1)
                        else:
                            uk_ok.wait(e, c - 1, d - 1)
                        move("CV", d, i, xs[:, d, :], bias=cb[:, d:d + 1])
                return job

            def front_silus(c, i):
                halo_ok.by(e.activation(xpre[:, :, 0:HALO], xpre[:, :, TC:TC + HALO], ACT.Copy))
                e.preload_act_table(ACT.Silu)
                halo_ok.wait(e, c)
                xs_ok.by(e.activation(xs[:, :, :], xs[:, :, :], ACT.Silu))
                xs_ok.by(e.activation(sres_n[:, :, :], sres_n[:, :, :], ACT.Silu))
                e.preload_act_table_set(LOG_EXP)

            def dt_raw(d):
                return lambda c, i: move("DT", d, i, xpre[:, d, HALO:HALO + TC])

            def softplus(d):
                def job(c, i):
                    e_ok.wait(e, c - 1, GPD * NG * (d + 1))
                    if d < 2:
                        u_ok.wait(e, c - 1, d + 1)
                    else:
                        uk_ok.wait(e, c - 1, d - 1)
                    if d < ND - 1:
                        wait_read(e, i, "DT", d)
                    else:
                        wait_read(e, i - 1, "SP", 2 * N - 1)
                    soft.by(e.activation(dt_[:, d, :], xpre[:, d, HALO:HALO + TC], ACT.Abs))
                    soft.wait(e, c, 3 * d + 1)
                    soft.by(e.activation(dt_[:, d, :], dt_[:, d, :], ACT.Exp, scale=-1.0))
                    soft.wait(e, c, 3 * d + 2)
                    soft.by(e.activation(dt_[:, d, :], dt_[:, d, :], ACT.Ln, bias=1.0))
                return job

            def spread(g, late):
                def job(c, i):
                    bu_ok.wait(e, c - 1, Q - GPD + (g + 1) * SG // NG)
                    ch_ok.wait(e, c - 1, 2 * (Q - GPD + (g + 1) * SG // NG))
                    for k in range(2 * SG):
                        dst = (b_all, c_all)[k // SG]
                        move("SP", 2 * SG * g + k, i - late, dst[:, SG * g + k % SG, :])
                return job

            def res_on(c, i):
                xs_ok.wait(e, c)
                if has_back(i):
                    wait_full(e, i, "M", NT // 2 - 1)
                sr_ok.by(e.activation(sres[:, :, :], sres_n[:, :, :], ACT.Copy))

            def residual(c, i):
                x1_in.wait(e, c)
                kept_ok.wait(e, i, 1)
                for b in range(NT):
                    x1a_ok.by(e.activation(x1[:, b, :], x1[:, b, :], ACT.Identity,
                                           bias=kept[:, 1, 0, b:b + 1], scale=kept[:, 1, 1, b:b + 1]))

            def normal2(c, i):
                scales2.wait(e, c)
                for b in range(NT):
                    xn2_ok.by(e.activation(xn2[:, b, :], x1[:, b, :], ACT.Identity,
                                           bias=st2[:, 3, b:b + 1], scale=st2[:, 1, b:b + 1]))

            def gate(*fs):
                def job(c, i):
                    for f in fs:
                        move("GATE", f, i, hb[:, f, :])
                return job

            def tails(c, i):
                bank = wait_full(e, i, "TAIL", 0)
                silu_ok.by(e.activation(hb[FR:P, FT, :], bank[0:FR, :], ACT.Copy))
                read_out(e.activation(up_t[FR:P, :], bank[FR:P, :], ACT.Copy), "TAIL", 0)

            def gate_silus(c, i):
                e.preload_act_table(ACT.Silu)
                wait_read(e, i, "TAIL", 0)
                silu_ok.by(e.activation(hb[:, 0:FT, :], hb[:, 0:FT, :], ACT.Silu))
                silu_ok.by(e.activation(hb[FR:P, FT, :], hb[FR:P, FT, :], ACT.Silu))
                e.preload_act_table_set(LOG_EXP)

            G = N // SG
            table = [(0, "scan", spread(G - 2, 1)), (2, "scan", spread(G - 1, 1)), (2, "front", normal),
                     (3, "back", residual), (3, "scan", softplus(ND - 1)), (4, "front", turned("XT")), (5, "scan", res_on),
                     (6, "front", before_conv(0, 1)), (7, "front", before_conv(2, 3)), (8, "front", res(0, 1)), (9, "front", res(2, 3)),
                     (10, "back", normal2), (10, "front", convolved(0)), (11, "front", convolved(1)), (11, "back", turned("OXT")),
                     (12, "front", convolved(2)), (13, "front", convolved(3)), (13, "front", front_silus),
                     (14, "back", gate(0, 1)), (15, "back", gate(2, 3)), (16, "back", gate(4)), (16, "back", tails),
                     (17, "front", dt_raw(0)), (17, "front", softplus(0)), (18, "front", dt_raw(1)), (18, "front", softplus(1)),
                     (19, "back", gate_silus), (20, "front", dt_raw(2)), (21, "front", dt_raw(3)), (25, "front", softplus(2)),
                     (29, "front", spread(0, 0)), (31, "front", spread(1, 0))]
            run(e, table, group)

        @block.tensor
        def _(e):
            def product(out_ap, terms):
                for n, (a, b) in enumerate(terms):
                    last = e.matmul(out_ap, a, b, start=(n == 0), stop=(n == len(terms) - 1))
                return last

            def cols(n):
                return slice(n * P, (n + 1) * P)

            e.wait_ge(s_id, POOL_CONSTS)
            e.wait_ge(s_ld[1], 16)
            for j in range(ND):
                for k in range(ND):
                    last = e.transpose(gbank[j][:, cols(k)], wx_ld[:, k, cols(j)], ident[:, :])
                last.then_inc(s_tr, 1)
            e.wait_ge(s_ld[2], 16)
            e.wait_ge(s_tc, ND)
            for k in range(ND):
                product(gbank[k][:, :], [(wxT[:, j, cols(k)], wdt_ld[:, j, :]) for j in range(ND)]).then_inc(s_tr, 1)
            e.wait_ge(s_tc, 2 * ND)
            e.wait_ge(s_c, DVE_CONSTS)
            e.wait_ge(s_ca, 2)

            def group(c, q):
                if q % GPD == 0:
                    yg_ok.wait(e, c, q // GPD)
                ch_ok.wait(e, c, 2 * (q + 1))
                y_ok.by(e.matmul(ybank[:, :], ident[:, :], ring[:, q % RING, 0, :],
                                 start=(q % GPD == 0), stop=(q % GPD == GPD - 1)))

            def turn(name, src, done):
                def job(c, i):
                    done.wait(e, c)
                    for k in range(KD):
                        bank = wait_free(e, i, name, k)
                        for b in range(NT):
                            last = e.transpose(bank[:, cols(b)], src[:, b, cols(k)], ident[:, :])
                        filled(last, name, k)
                return job

            def project_in(name, *ds):
                def job(c, i):
                    if (name, ds[0]) == ("IN", 0):
                        for k in range(KD):
                            wait_read(e, i, "XT", k)
                    for d in ds:
                        m = d + (ND if name == "RES" else 0)
                        bank = wait_free(e, i, name, d)
                        filled(product(bank[:, :], [(win[:, k, cols(m)], xT[:, k, :]) for k in range(KD)]), name, d)
                return job

            def convolve(d):
                def job(c, i):
                    if d >= 2:
                        wait_read(e, i, "IN", d)
                    bank = wait_free(e, i, "CV", d)
                    filled(product(bank[:, :], [(cdiag[:, d, k, :], xpre[:, d, k:k + TC]) for k in range(TAPS)]), "CV", d)
                return job

            def bc(c, i):
                xs_ok.wait(e, c, 1)
                bank = wait_free(e, i, "BC", 0)
                filled(product(bank[0:3 * W, :], [(wbc[:, k, :, :].rearrange("p r n -> p (r n)"), xs[:, k, :]) for k in range(ND)]), "BC", 0)

            def dt_in(d):
                def job(c, i):
                    bank = wait_free(e, i, "DT", d)
                    filled(product(bank[:, :], [(wc[:, k, cols(d)], xs[:, k, :]) for k in range(ND)]), "DT", d)
                return job

            def spread(g):
                def job(c, i):
                    bc_ok.wait(e, c)
                    for k in range(2 * SG):
                        n = k // SG * N + SG * g + k % SG
                        bank = wait_free(e, i, "SP", 2 * SG * g + k)
                        filled(e.matmul(bank[:, :], pick[:, n:n + 1].broadcast_to([3 * W, P]), bc_s[:, :], start=True, stop=True),
                               "SP", 2 * SG * g + k)
                return job

            def project(t):
                def job(c, i):
                    yg_ok.wait(e, c)
                    bank = wait_free(e, i, "M", t)
                    for b in range(2):
                        last = product(bank[:, b * D:(b + 1) * D], [(sres[:, k, cols(2 * t + b)], wout[:, k, :]) for k in range(ND)])
                    filled(last, "M", t)
                return job

            def expand(name, *fs):
                def job(c, i):
                    if (name, fs[0]) == ("GATE", 0):
                        w13_in.wait(e, c)
                        for k in range(KD):
                            wait_read(e, i, "OXT", k)
                    for f in fs:
                        bank = wait_free(e, i, name, f)
                        filled(product(bank[:, :], [(w13[:, k, int(name == "UP"), cols(f)], xT[:, k, :]) for k in range(KD)]), name, f)
                return job

            def tail(c, i):
                bank = wait_free(e, i, "TAIL", 0)
                filled(product(bank[:, :], [(w13t[:, k, :], xT[:, k, :]) for k in range(KD)]), "TAIL", 0)

            def contract(t):
                def job(c, i):
                    w2_in.wait(e, c)
                    tail_ok.wait(e, c)
                    for f in range(FT - NB, FT):
                        wait_read(e, i, "UP", f)
                    bank = gbank[POS["DOWN", t] % NB]
                    for b in range(2):
                        tok = cols(2 * t + b)
                        last = product(bank[:, b * D:(b + 1) * D], [(hb[:, f, tok], w2s[:, f, :]) for f in range(FT)]
                                       + [(hb[FR:P, FT, tok], w2s[FR:P, FT, :])])
                    filled(last, "DOWN", t)
                return job

            table = [(0, "back", project(0)), (1, "back", project(1)), (2, "front", turn("XT", xin, xn_ok)),
                     (3, "front", project_in("IN", 0, 1)), (4, "front", project_in("IN", 2, 3)),
                     (5, "front", project_in("RES", 0, 1)), (6, "front", project_in("RES", 2, 3)),
                     (7, "front", convolve(0)), (8, "front", convolve(1)), (9, "back", turn("OXT", xn2, xn2_ok)),
                     (9, "front", convolve(2)), (10, "front", convolve(3)),
                     (11, "back", expand("GATE", 0, 1)), (12, "back", expand("GATE", 2, 3)), (13, "back", expand("GATE", 4)),
                     (13, "back", tail), (14, "front", bc), (15, "front", dt_in(0)), (16, "front", dt_in(1)),
                     (17, "front", dt_in(2)), (18, "front", dt_in(3)), (19, "back", expand("UP", 0, 1)),
                     (20, "back", expand("UP", 2, 3)), (21, "back", expand("UP", 4)), (22, "back", contract(0)), (24, "back", contract(1)),
                     (27, "front", spread(0)), (29, "front", spread(1)), (30, "front", spread(2)), (31, "front", spread(3))]
            run(e, table, group)


_INS = ["L0_attn_x", "L0_attn_rms_w", "L0_attn_W_in", "L0_attn_conv_w", "L0_attn_conv_b", "L0_attn_W_x", "L0_attn_W_dt",
        "L0_attn_A_log", "L0_attn_W_out", "L0_ffn_w1", "L0_ffn_w3", "L0_ffn_w2"]


def kernel(**inputs):
    import numpy as _np
    import concourse.bacc as _bacc
    from concourse import mybir as _mybir
    from concourse.bass_utils import run_bass_kernel_spmd as _run

    nc = _bacc.Bacc("TRN2", target_bir_lowering=False, num_devices=1)
    arrays, args = {}, []
    for name in _INS:
        a = _np.ascontiguousarray(inputs[name])
        arrays[f"in_{name}_dram"] = a
        args.append(nc.dram_tensor(f"in_{name}_dram", a.shape, _mybir.dt.from_np(a.dtype), kind="ExternalInput").ap())
    shape = inputs["L0_attn_x"].shape
    args.append(nc.dram_tensor("out_dram", shape, f32, kind="ExternalOutput").ap())
    mamba_moe_layer(nc, *args)
    r = _run(nc, [arrays], core_ids=[0])
    return r.results[0]["out_dram"]
```

```python
import concourse.bass as bass
from concourse import mybir
from contextlib import ExitStack

f32 = mybir.dt.float32
bf16 = mybir.dt.bfloat16
ALU = mybir.AluOpType
ACT = mybir.ActivationFunctionType


def mamba_moe_layer(nc, x, rms_w, W_in, conv_w, conv_b, W_x, W_dt, A_log, W_out, w1, w3, w2, out):
    T, D = x.shape[1], x.shape[2]
    DI, N = A_log.shape
    TAPS = conv_w.shape[2]
    E, _, FF = w1.shape
    P = 128
    TC = T // E
    NT = TC // P
    KD = D // P
    ND = DI // P
    HALO = TAPS - 1
    NG = 2
    GPD = N // NG
    Q = ND * GPD
    NS = Q * NG
    RING = 4
    SUMS = 4
    LAG = 4
    OWN = (9, 26)
    SG = 4
    FT = FF // P
    FR = FF - FT * P
    W = 2 * N
    assert min(OWN) >= GPD and FR * 2 == P and Q % RING == 0 and Q % SUMS == 0 and TC == 512 and 3 * W <= P
    EPS = 1e-5

    ctx = ExitStack()
    with ctx:
        def sb(name, shape, dt=f32):
            return ctx.enter_context(nc.sbuf_tensor(name, shape, dt))

        def pb(name):
            return ctx.enter_context(nc.psum_tensor(name, [P, TC], f32))

        def sem(name):
            return ctx.enter_context(nc.semaphore(name))

        b_all = sb("b_all", [P, N, TC])
        c_all = sb("c_all", [P, N, TC])
        ring = sb("ring", [P, RING, NG, TC])
        sums = sb("sums", [P, SUMS, TC])
        dt_ = sb("dt_", [P, ND, TC])
        xs = sb("xs", [P, ND, TC])
        u_kept = sb("u_kept", [P, ND - 2, TC])
        sres_n = sb("sres_n", [P, ND, TC])
        sres = sb("sres", [P, ND, TC])
        xin = sb("xin", [P, NT, D])
        xT = sb("xT", [P, KD, TC])
        xpre = sb("xpre", [P, ND, HALO + TC])
        hb = sb("hb", [P, FT + 1, TC])
        x1 = sb("x1", [P, NT, D])
        xn2 = sb("xn2", [P, NT, D])
        bc_s = sb("bc_s", [3 * W, TC], bf16)
        win = sb("win", [P, KD, 2 * DI])
        wc = sb("wc", [P, ND, DI])
        wbc = sb("wbc", [P, ND, 3, W])
        wout = sb("wout", [P, ND, D])
        cdiag = sb("cdiag", [P, ND, TAPS - 1, P])
        w13 = sb("w13", [P, KD, 2, FT * P])
        w13t = sb("w13t", [P, KD, P])
        w2s = sb("w2s", [P, FT + 1, D])
        ident = sb("ident", [P, P])
        pick = sb("pick", [3 * W, W], bf16)
        a_neg = sb("a_neg", [P, ND, N])
        cw = sb("cw", [P, ND, TAPS])
        cb = sb("cb", [P, ND])
        rw = sb("rw", [P, KD])
        state = sb("state", [P, Q, NG])
        bn = sb("bn", [P, NT, 6])
        mv = sb("mv", [P, NT, 2])
        bn2 = sb("bn2", [P, NT, 6])
        mv2 = sb("mv2", [P, NT, 2])
        st = sb("st", [P, 11, NT])
        kept = sb("kept", [P, 2, 2, NT])
        st2 = sb("st2", [P, 4, NT])
        consts = sb("consts", [P, 6, NT])
        taken = sb("taken", [1, 1])
        bc_r = xn2[0:3 * W, 0:NT // 2, :].rearrange("p b d -> p (b d)")
        up_t = xn2[:, NT // 2:NT, :].rearrange("p b d -> p (b d)")
        wx_ld = hb[:, :, :].rearrange("p a b -> p (a b)")[:, 0:ND * (DI + W)].rearrange("p (k n) -> p k n", k=ND)
        wxT = ring[:, :, :, :].rearrange("p r g t -> p (r g) t")[:, 0:ND, :]
        wdt_ld = ring[:, :, :, :].rearrange("p r g t -> p (r g) t")[:, ND:2 * ND, :]

        ubank = pb("ubank")
        ybank = pb("ybank")
        ebank = [pb("ebank0"), pb("ebank1")]
        gbank = [pb(f"gbank{b}") for b in range(4)]
        NB = len(gbank)

        PLAN = [
            (0, "front", "XT", 0), (1, "scan", "SP", 4), (1, "front", "IN", 0), (1, "front", "IN", 1),
            (2, "scan", "SP", 5), (3, "scan", "SP", 6), (4, "front", "IN", 2), (5, "front", "IN", 3),
            (5, "back", "M", 0), (5, "scan", "SP", 7), (5, "back", "M", 1), (7, "front", "CV", 0),
            (9, "front", "RES", 0), (9, "front", "CV", 1), (10, "front", "RES", 1), (10, "front", "RES", 2),
            (11, "front", "CV", 2), (11, "front", "RES", 3), (11, "front", "CV", 3), (11, "back", "OXT", 0),
            (13, "back", "GATE", 0), (13, "back", "GATE", 1), (13, "back", "GATE", 2), (13, "back", "GATE", 3),
            (15, "back", "GATE", 4), (15, "back", "TAIL", 0), (17, "front", "BC", 0), (19, "back", "UP", 0),
            (19, "front", "DT", 0), (19, "back", "UP", 1), (19, "back", "UP", 2), (22, "front", "DT", 1),
            (23, "back", "UP", 3), (23, "back", "UP", 4), (25, "front", "DT", 2), (25, "back", "DOWN", 0),
            (26, "back", "DOWN", 1), (27, "front", "DT", 3), (28, "front", "SP", 0), (29, "front", "SP", 2),
            (31, "front", "SP", 1), (31, "front", "SP", 3)]
        BANKS = {"XT": KD, "OXT": KD, "SP": SG}
        USES = [(name, k * BANKS.get(name, 1) + j) for _, _, name, k in PLAN for j in range(BANKS.get(name, 1))]
        SPREADS = [(0, 0), (0, 1), (1, 0), (1, 1), (0, 2), (0, 3), (1, 2), (1, 3)]
        assert len(USES) % NB == 0
        PER = len(USES) // NB
        POS = {use: p for p, use in enumerate(USES)}
        OF_BACK = tuple({name for _, part, name, _ in PLAN if part == "back"})
        full = [sem(f"full{b}") for b in range(NB)]
        free = [sem(f"free{b}") for b in range(NB)]

        def known(i):
            return isinstance(i, int)

        def has_front(i):
            return not known(i) or i < E - 1

        def has_scan(i):
            return not known(i) or 0 <= i < E

        def has_back(i):
            return not known(i) or i >= 1

        def has_next(i):
            return not known(i) or i < E - 2

        def of_scan(use):
            return use[0] == "SP" and use[1] >= N

        def there(use, i):
            return has_scan(i) if of_scan(use) else has_back(i) if use[0] in OF_BACK else has_front(i)

        def uses_of(b, i, before=len(USES)):
            return sum(there(USES[p], i) for p in range(b, before, NB))

        assert all(POS["SP", k] > POS[use] for k in range(N) for use in USES if use[0] in OF_BACK)
        lacking = [2 * PER - uses_of(b, -1) - uses_of(b, 0) for b in range(NB)]

        def nth(i, name, k):
            p = POS[name, k]
            b = p % NB
            if known(i):
                return b, lacking[b] + sum(uses_of(b, j) for j in range(-1, i)) + uses_of(b, i, p) + 1
            return b, (i + 1) * PER + p // NB + 1

        def wait_full(e, i, name, k):
            b, n = nth(i, name, k)
            e.wait_ge(full[b], n)
            return gbank[b]

        def wait_read(e, i, name, k):
            b, n = nth(i, name, k)
            e.wait_ge(free[b], n)

        def wait_read_before(e, i, name, k, to):
            if POS[name, k] % NB != POS[to] % NB:
                wait_read(e, i, name, k)

        def wait_free(e, i, name, k):
            b, n = nth(i, name, k)
            e.wait_ge(free[b], n - 1)
            return gbank[b]

        def wait_spread(e, c, which, n):
            k = SPREADS.index((which, n // SG)) * SG + n % SG
            wait_read(e, c if k >= N else c - 1, "SP", k)

        def filled(ins, name, k):
            ins.then_inc(full[POS[name, k] % NB], 1)

        def read_out(ins, name, k):
            ins.then_inc(free[POS[name, k] % NB], 1)

        events = []

        class Event:
            def __init__(self, name, number):
                self.sem, self.number = sem("s_" + name), number
                events.append(self)

            def wait(self, e, c, j=None):
                n = (c + 1) * self.number + (self.number if j is None else j)
                if not known(n) or n > self.number:
                    e.wait_ge(self.sem, n)

            def by(self, ins):
                ins.then_inc(self.sem, 1)

        x_in, x1_in, w13_in, w2_in, stored = (Event(n, k) for n, k in (
            ("x_in", 16), ("x1_in", 16), ("w13_in", 64), ("w2_in", 32), ("stored", 16)))
        bn_ok = Event("bn_ok", 1)
        stats = Event("stats", 1)
        scales = Event("scales", 11)
        kept_ok = Event("kept_ok", 2)
        xn_ok = Event("xn_ok", NT)
        halo_ok = Event("halo_ok", 1)
        xs_ok = Event("xs_ok", ND + 1)
        soft = Event("soft", 3 * ND)
        dt_ok = Event("dt_ok", ND)
        bc_ok = Event("bc_ok", 4)
        u_ok = Event("u_ok", ND)
        uk_ok = Event("uk_ok", ND - 2)
        sr_ok = Event("sr_ok", 1)
        bu_ok = Event("bu_ok", Q)
        e_ok = Event("e_ok", NS)
        h_ok = Event("h_ok", NS)
        st_ok = Event("st_ok", Q)
        ch_ok = Event("ch_ok", 2 * (Q - len(OWN)))
        cho_ok = Event("cho_ok", 2 * len(OWN))
        y_ok = Event("y_ok", Q)
        yg_ok = Event("yg_ok", ND)
        x1a_ok = Event("x1a_ok", NT)
        bn2_ok = Event("bn2_ok", 1)
        stats2 = Event("stats2", 1)
        scales2 = Event("scales2", 4)
        xn2_ok = Event("xn2_ok", NT)
        silu_ok = Event("silu_ok", 3)
        tail_ok = Event("tail_ok", 1)

        def wait_ch(e, c, q):
            own = sum(o <= q for o in OWN)
            if q in OWN:
                cho_ok.wait(e, c, 2 * own)
            else:
                ch_ok.wait(e, c, 2 * (q + 1 - own))

        s_ld = [sem(f"s_ld{n}") for n in range(5)]
        s_id = sem("s_id")
        s_c = sem("s_c")
        s_ca = sem("s_ca")
        s_tr = sem("s_tr")
        s_tc = sem("s_tc")
        POOL_CONSTS, DVE_CONSTS = 17, KD + ND * (TAPS - 1)
        spare = (ubank, ybank, *ebank)

        block = ctx.enter_context(nc.Block())

        def rows(t, c):
            return t[0, bass.ds(c * TC, TC), :].rearrange("(b p) d -> p b d", p=P)

        def run(e, table, group=None, before=None, always=False):
            def iteration(i):
                on = {"next": (has_next(i), i + 2), "handed": (not known(i) or i < E, i + 1), "front": (has_front(i), i + 1),
                      "set-up": (known(i) and i == -1, 0), "scan": (has_scan(i), i), "back": (has_back(i), i - 1)}
                if has_scan(i) and before:
                    before(i)
                for q in range(Q):
                    if group and (always or has_scan(i)):
                        group(i, q)
                    for at, part, job in table:
                        if at == q and on[part][0]:
                            job(on[part][1], i)

            for _, part, job in table:
                if part == "next":
                    job(0, -2)
            iteration(-1)
            iteration(0)
            with e.Fori(1, E - 2) as i:
                iteration(i)
            for i in range(E - 2, E + 1):
                iteration(i)

        @block.sync
        def _(e):
            for ev in events:
                e.sem_inc(ev.sem, ev.number)
            for b in range(NB):
                e.sem_inc(full[b], lacking[b])
                e.sem_inc(free[b], lacking[b])

            def load_x(c):
                e.dma_start(xin[:, :, :], rows(x, c)).then_inc(x_in.sem, 16)

            def load_x1(c):
                e.dma_start(x1[:, :, :], rows(x, c)).then_inc(x1_in.sem, 16)

            def load_w13(c):
                for j, w in enumerate((w1, w3)):
                    src = w[bass.ds(c, 1), :, :].rearrange("a (k p) f -> p (a k) f", p=P)
                    e.dma_start(w13[:, :, j, :], src[:, :, 0:FT * P]).then_inc(w13_in.sem, 16)
                    e.dma_start(w13t[:, :, j * FR:(j + 1) * FR], src[:, :, FT * P:FF]).then_inc(w13_in.sem, 16)

            def load_w2(c):
                e.dma_start(w2s[:, 0:FT, :], w2[bass.ds(c, 1), 0:FT * P, :].rearrange("a (k p) d -> p (a k) d", p=P)).then_inc(w2_in.sem, 16)
                e.dma_start(w2s[P - FR:P, FT:FT + 1, :], w2[bass.ds(c, 1), FT * P:FF, :].rearrange("a p d -> p a d")).then_inc(w2_in.sem, 16)

            load_x(0)
            e.dma_start(cw[:, :, :], conv_w.rearrange("(d p) a k -> p d (a k)", p=P)).then_inc(s_ld[0], 16)
            e.dma_start(cb[:, :], conv_b.rearrange("(d p) -> p d", p=P), allow_slow_non_contiguous=True).then_inc(s_ld[0], 16)
            e.dma_start(rw[:, :], rms_w.rearrange("(d p) -> p d", p=P), allow_slow_non_contiguous=True).then_inc(s_ld[0], 16)
            e.dma_start(a_neg[:, :, :], A_log.rearrange("(d p) n -> p d n", p=P)).then_inc(s_ld[0], 16)
            e.dma_start(win[:, :, :], W_in.rearrange("(k p) n -> p k n", p=P)).then_inc(s_ld[3], 16)
            e.dma_start(wx_ld, W_x.rearrange("(k p) n -> p k n", p=P)).then_inc(s_ld[1], 16)
            e.dma_start(wdt_ld, W_dt.rearrange("(k p) n -> p k n", p=P)).then_inc(s_ld[2], 16)
            e.dma_start(wout[:, :, :], W_out.rearrange("(k p) n -> p k n", p=P)).then_inc(s_ld[4], 16)
            load_x1(0)
            load_w13(0)
            load_w2(0)

            def next_x(i):
                xs_ok.wait(e, i + 1, ND)
                load_x(i + 2)

            def back(i):
                if not known(i) or i < E:
                    wait_full(e, i, "UP", FT - 1)
                    load_w13(i)
                    wait_full(e, i, "DOWN", NT // 2 - 1)
                    load_w2(i)
                wait_read(e, i, "DOWN", NT // 2 - 1)
                e.dma_start(rows(out, i - 1), x1[:, :, :]).then_inc(stored.sem, 16)
                stored.wait(e, i - 1)
                if not known(i) or i < E:
                    load_x1(i)

            next_x(-1)
            next_x(0)
            with e.Fori(1, E - 2) as i:
                next_x(i)
                back(i)
            for i in range(E - 2, E + 1):
                back(i)

        @block.gpsimd
        def _(e):
            made = [0]

            def step(ins):
                made[0] += 1
                ins.then_inc(s_id, 1)
                e.wait_ge(s_id, made[0])

            step(e.memset(ident[:, :], 0.0))
            step(e.affine_select(out=ident[:, :], in_=ident[:, :], compare_op=ALU.not_equal, fill=1.0,
                                 base=0, pattern=[[-1, P]], channel_multiplier=1))
            for n, value in enumerate((-0.5, EPS, -1.0, 1.0, 0.0, 0.0)):
                step(e.memset(consts[:, n, :], value))
            step(e.memset(pick[:, :], 0.0))
            step(e.memset(state[:, :, :], 0.0))
            step(e.memset(xpre[:, :, 0:HALO], 0.0))
            step(e.memset(st[:, :, :], 0.0))
            step(e.memset(kept[:, :, :, :], 0.0))
            for r in range(3):
                step(e.affine_select(out=pick[:, :], in_=pick[:, :], compare_op=ALU.not_equal, fill=1.0,
                                     base=-r * W, pattern=[[-1, W]], channel_multiplier=1))
            step(e.memset(taken[:, :], 0.0))
            assert made[0] == POOL_CONSTS
            mhalf, eps, minus, one, zero = (consts[:, n, :] for n in range(5))
            zeros = consts[:, 4:6, :]

            def hand_on(c, i):
                if not known(c) or c < E:
                    scales.wait(e, c)
                x1a_ok.wait(e, c - 2)
                kept_ok.by(e.tensor_tensor(kept[:, 1, :, :], kept[:, 0, :, :], zeros, ALU.add))
                kept_ok.wait(e, c, 1)
                if not known(c) or c < E:
                    kept_ok.by(e.tensor_tensor(kept[:, 0, :, :], st[:, 9:11, :], zeros, ALU.add))

            def front(c, i):
                j = [0]

                def then(ins):
                    j[0] += 1
                    scales.by(ins)
                    scales.wait(e, c, j[0])

                m, v = mv[:, :, 0], mv[:, :, 1]
                ve, r, vr, ms, mse, r2, s, nm, bs, br, rp = (st[:, n, :] for n in range(11))
                stats.wait(e, c)
                xn_ok.wait(e, c - 1)
                kept_ok.wait(e, c - 1)
                then(e.tensor_tensor(ve, v, eps, ALU.add))
                then(e.tensor_tensor(r, ve, mhalf, ALU.pow))
                then(e.tensor_tensor(vr, v, r, ALU.mult))
                then(e.tensor_tensor(ms, vr, r, ALU.mult))
                then(e.tensor_tensor(mse, ms, eps, ALU.add))
                then(e.tensor_tensor(r2, mse, mhalf, ALU.pow))
                then(e.tensor_tensor(s, r, r2, ALU.mult))
                then(e.tensor_tensor(nm, m, minus, ALU.mult))
                then(e.tensor_tensor(bs, nm, s, ALU.mult))
                then(e.tensor_tensor(br, nm, r, ALU.mult))
                then(e.tensor_tensor(rp, r, one, ALU.add))

            def group(c, q):
                if q in OWN:
                    return
                slot, n = ring[:, q % RING, :, :], q % GPD * NG
                st_ok.wait(e, c, q + 1)
                if q < GPD:
                    for k in range(n, n + NG):
                        wait_spread(e, c, 1, k)
                ch_ok.by(e.tensor_tensor(slot, slot, c_all[:, n:n + NG, :], ALU.mult))
                ch_ok.wait(e, c, 2 * (q - sum(o < q for o in OWN)) + 1)
                y_ok.wait(e, c, q - SUMS + 1)
                ch_ok.by(e.tensor_tensor(sums[:, q % SUMS, :], slot[:, 0, :], slot[:, 1, :], ALU.add))

            def back(c, i):
                def then(ins, j):
                    scales2.by(ins)
                    scales2.wait(e, c, j)

                stats2.wait(e, c)
                xn2_ok.wait(e, c - 1)
                then(e.tensor_tensor(st2[:, 0, :], mv2[:, :, 1], eps, ALU.add), 1)
                then(e.tensor_tensor(st2[:, 1, :], st2[:, 0, :], mhalf, ALU.pow), 2)
                then(e.tensor_tensor(st2[:, 2, :], mv2[:, :, 0], minus, ALU.mult), 3)
                then(e.tensor_tensor(st2[:, 3, :], st2[:, 2, :], st2[:, 1, :], ALU.mult), 4)

            table = [(9, "back", back), (21, "handed", hand_on), (21, "next", front)]
            run(e, table, group)

        @block.vector
        def _(e):
            def scale_weights():
                e.wait_ge(s_ld[0], 64)
                e.wait_ge(s_ld[3], 16)
                for k in range(KD):
                    e.tensor_scalar(win[:, k, :], win[:, k, :], rw[:, k:k + 1], None, ALU.mult).then_inc(s_c, 1)
                for d in range(ND):
                    for k in range(TAPS - 1):
                        e.tensor_scalar(cdiag[:, d, k, :], ident[:, :], cw[:, d, k:k + 1], None, ALU.mult).then_inc(s_c, 1)

            def weights_x(c, i):
                e.wait_ge(s_ld[1], 16)
                for r in range(3):
                    e.tensor_copy(wbc[:, :, r, :], wx_ld[:, :, DI:DI + W]).then_inc(s_tc, 1)
                for j in range(ND):
                    e.wait_ge(s_tr, j + 1)
                    e.tensor_copy(wxT[:, j, :], spare[j][:, :]).then_inc(s_tc, 1)
                for k in range(ND):
                    e.wait_ge(s_tr, ND + k + 1)
                    e.tensor_copy(wc[:, k, :], spare[k][:, :]).then_inc(s_tc, 1)

            def take():
                e.tensor_copy(taken[:, :], ident[0:1, 0:1])

            def row_stats(c, src, tmp, dst, first, second):
                for b in range(NT):
                    last = e.bn_stats(tmp[:, b, :], src[:, b, :])
                first.by(last)
                first.wait(e, c)
                take()
                for b in range(NT):
                    last = e.bn_aggr(dst[:, b, :], tmp[:, b, :])
                second.by(last)

            def x_stats(c, i):
                x_in.wait(e, c)
                stats.wait(e, c - 1)
                scales.wait(e, c - 1)
                row_stats(c, xin, bn, mv, bn_ok, stats)

            def split_bc(c, i):
                bank = wait_full(e, i, "BC", 0)
                bc_ok.wait(e, c - 1)
                bc_ok.by(e.tensor_copy(bc_s[:, :], bank[0:3 * W, :]))
                bc_ok.wait(e, c, 1)
                read_out(e.tensor_tensor(bc_r, bank[0:3 * W, :], bc_s[:, :], ALU.subtract), "BC", 0)
                wait_read(e, i, "BC", 0)
                for r in (1, 2):
                    bc_ok.by(e.tensor_copy(bc_s[r * W:(r + 1) * W, :], bc_r[r * W:(r + 1) * W, :]))
                bc_ok.wait(e, c, 3)
                third = slice(2 * W, 3 * W)
                bc_ok.by(e.tensor_tensor(bc_s[third, :], bc_r[third, :], bc_s[third, :], ALU.subtract))

            def dt_of(d):
                def job(c, i):
                    soft.wait(e, c, 3 * (d + 1))
                    dt_ok.by(e.scalar_tensor_tensor(dt_[:, d, :], xpre[:, d, HALO:HALO + TC], 0.0, dt_[:, d, :], ALU.max, ALU.add))
                return job

            def convolved(d):
                def job(c, i):
                    if d < 2:
                        u_ok.wait(e, c - 1, d + 1)
                    else:
                        uk_ok.wait(e, c - 1, d - 1)
                    bank = wait_full(e, i, "CV", d)
                    read_out(e.scalar_tensor_tensor(xs[:, d, :], xpre[:, d, HALO:HALO + TC], cw[:, d, HALO:TAPS], bank[:, :], ALU.mult, ALU.add),
                             "CV", d)
                return job

            def keep_u(c, i):
                dt_ok.wait(e, c)
                u_ok.wait(e, c - 1)
                for d in range(2, ND):
                    uk_ok.by(e.tensor_tensor(u_kept[:, d - 2, :], dt_[:, d, :], xs[:, d, :], ALU.mult))

            def u_of(c, d):
                bu_ok.wait(e, c, d * GPD)
                if d < 2:
                    dt_ok.wait(e, c, d + 1)
                    xs_ok.wait(e, c, ND)
                    u_ok.by(e.tensor_tensor(ubank[:, :], dt_[:, d, :], xs[:, d, :], ALU.mult))
                else:
                    uk_ok.wait(e, c, d - 1)
                    u_ok.by(e.tensor_copy(ubank[:, :], u_kept[:, d - 2, :]))

            def bu(c, q):
                n = q % GPD * NG
                u_ok.wait(e, c, q // GPD + 1)
                wait_ch(e, *((c, q - RING) if q >= RING else (c - 1, q - RING + Q)))
                if q < GPD:
                    for k in range(n, n + NG):
                        wait_spread(e, c, 0, k)
                bu_ok.by(e.tensor_tensor(ring[:, q % RING, :, :], b_all[:, n:n + NG, :],
                                         ubank[:, :].unsqueeze(1).broadcast_to([P, NG, TC]), ALU.mult))

            def start(c):
                u_of(c, 0)
                bu(c, 0)

            def group(c, q):
                bu_ok.wait(e, c, q + 1)
                st_ok.wait(e, c - 1, q + 1)
                for n in range(NG):
                    j = q * NG + n
                    e_ok.wait(e, c, j + 1)
                    row = ring[:, q % RING, n, :]
                    h_ok.by(e.tensor_tensor_scan(row, ebank[j % 2][:, :], row, initial=state[:, q, n:n + 1],
                                                 op0=ALU.mult, op1=ALU.add))
                if q + 1 < Q:
                    if (q + 1) % GPD == 0:
                        u_of(c, (q + 1) // GPD)
                    bu(c, q + 1)
                h_ok.wait(e, c, NG * (q + 1))
                st_ok.by(e.tensor_copy(state[:, q, :], ring[:, q % RING, :, TC - 1]))
                if q in OWN:
                    slot, n = ring[:, q % RING, :, :], q % GPD * NG
                    if q == OWN[0]:
                        wait_read(e, c, "SP", 2 * N - 1)
                    st_ok.wait(e, c, q + 1)
                    cho_ok.by(e.tensor_tensor(slot, slot, c_all[:, n:n + NG, :], ALU.mult))
                    cho_ok.wait(e, c, 2 * OWN.index(q) + 1)
                    y_ok.wait(e, c, q - SUMS + 1)
                    cho_ok.by(e.tensor_tensor(sums[:, q % SUMS, :], slot[:, 0, :], slot[:, 1, :], ALU.add))

            def gated(d):
                def job(c, i):
                    y_ok.wait(e, c, GPD * (d + 1))
                    sr_ok.wait(e, c)
                    yg_ok.by(e.tensor_tensor(sres[:, d, :], ybank[:, :], sres[:, d, :], ALU.mult))
                return job

            def add_rows(name, t, ready):
                def job(c, i):
                    bank = wait_full(e, i, name, t)
                    ready.wait(e, c)
                    two = x1[:, 2 * t:2 * t + 2, :]
                    read_out(e.tensor_tensor(two, two, bank[:, :].rearrange("p (b d) -> p b d", b=2), ALU.add), name, t)
                return job

            def x1_stats(c, i):
                for t in range(NT // 2):
                    wait_read(e, i, "M", t)
                stats2.wait(e, c - 1)
                scales2.wait(e, c - 1)
                row_stats(c, x1, bn2, mv2, bn2_ok, stats2)

            def hidden(f):
                def job(c, i):
                    silu_ok.wait(e, c, 2)
                    bank = wait_full(e, i, "UP", f)
                    read_out(e.tensor_tensor(hb[:, f, :], hb[:, f, :], bank[:, :], ALU.mult), "UP", f)
                return job

            def hidden_tail(c, i):
                silu_ok.wait(e, c, 3)
                wait_read(e, i, "TAIL", 0)
                tail_ok.by(e.tensor_tensor(hb[FR:P, FT, :], hb[FR:P, FT, :], up_t[FR:P, :], ALU.mult))

            e.wait_ge(s_id, POOL_CONSTS)
            table = [(0, "set-up", lambda c, i: scale_weights()), (14, "set-up", weights_x),
                     (LAG - 1, "back", gated(ND - 1)), (4, "scan", dt_of(ND - 1)), (5, "scan", keep_u),
                     (6, "back", add_rows("M", 0, x1a_ok)), (8, "back", add_rows("M", 1, x1a_ok)), (8, "back", x1_stats),
                     (8, "front", convolved(0)), (10, "front", convolved(1)), (12, "front", convolved(2)), (13, "front", convolved(3)),
                     (18, "front", split_bc), (21, "back", hidden_tail), (20, "back", hidden(0)), (22, "front", dt_of(0)),
                     (20, "back", hidden(1)), (21, "back", hidden(2)), (17, "next", x_stats), (22, "front", dt_of(1)),
                     (23, "back", hidden(3)), (23, "back", hidden(4)), (25, "front", dt_of(2)),
                     (26, "back", add_rows("DOWN", 0, xn2_ok)), (28, "back", add_rows("DOWN", 1, xn2_ok))]
            table += [(GPD * (d + 1) + LAG - 1, "scan", gated(d)) for d in range(ND - 1)]
            run(e, table, group, before=start)

        @block.scalar
        def _(e):
            LOG_EXP = "natural_log_exp_and_others"
            e.preload_act_table_set(LOG_EXP)
            e.wait_ge(s_ld[0], 64)
            e.activation(a_neg[:, :, :], a_neg[:, :, :], ACT.Exp).then_inc(s_ca, 1)
            e.wait_ge(s_ca, 1)
            e.activation(a_neg[:, :, :], a_neg[:, :, :], ACT.Copy, scale=-1.0).then_inc(s_ca, 1)
            e.wait_ge(s_ca, 2)
            e.wait_ge(s_id, POOL_CONSTS)

            def group(c, q):
                d = q // GPD
                dt_ok.wait(e, c, d + 1)
                for n in range(NG):
                    j = q * NG + n
                    h_ok.wait(e, c, j - 1)
                    k = q % GPD * NG + n
                    e_ok.by(e.activation(ebank[j % 2][:, :], dt_[:, d, :], ACT.Exp, scale=a_neg[:, d, k:k + 1]))

            def move(name, k, i, dst, bias=None):
                bank = wait_full(e, i, name, k)
                if bias is None:
                    ins = e.activation(dst, bank[:, :], ACT.Copy)
                else:
                    ins = e.activation(dst, bank[:, :], ACT.Identity, bias=bias)
                read_out(ins, name, k)

            def normal(c, i):
                scales.wait(e, c)
                for b in range(NT):
                    xn_ok.by(e.activation(xin[:, b, :], xin[:, b, :], ACT.Identity,
                                          bias=st[:, 8, b:b + 1], scale=st[:, 6, b:b + 1]))

            def turned(name):
                def job(c, i):
                    for k in range(KD):
                        move(name, k, i, xT[:, k, :])
                return job

            def before_conv(*ds):
                def job(c, i):
                    for d in ds:
                        dt_ok.wait(e, c - 1, d + 1)
                        move("IN", d, i, xpre[:, d, HALO:HALO + TC])
                return job

            def res(*ds):
                def job(c, i):
                    sr_ok.wait(e, c - 1)
                    for d in ds:
                        move("RES", d, i, sres_n[:, d, :])
                return job

            def front_silus(c, i):
                wait_read(e, i, "CV", ND - 1)
                halo_ok.by(e.activation(xpre[:, :, 0:HALO], xpre[:, :, TC:TC + HALO], ACT.Copy))
                e.preload_act_table(ACT.Silu)
                halo_ok.wait(e, c)
                for d in range(ND):
                    xs_ok.by(e.activation(xs[:, d, :], xs[:, d, :], ACT.Silu, bias=cb[:, d:d + 1]))
                xs_ok.by(e.activation(sres_n[:, :, :], sres_n[:, :, :], ACT.Silu))
                e.preload_act_table_set(LOG_EXP)

            def dt_raw(d):
                return lambda c, i: move("DT", d, i, xpre[:, d, HALO:HALO + TC])

            def softplus(d):
                def job(c, i):
                    e_ok.wait(e, c - 1, GPD * NG * (d + 1))
                    if d < 2:
                        u_ok.wait(e, c - 1, d + 1)
                    else:
                        uk_ok.wait(e, c - 1, d - 1)
                    if d < ND - 1:
                        wait_read(e, i, "DT", d)
                    else:
                        wait_read(e, i - 1, "SP", N - 1)
                    soft.by(e.activation(dt_[:, d, :], xpre[:, d, HALO:HALO + TC], ACT.Abs))
                    soft.wait(e, c, 3 * d + 1)
                    soft.by(e.activation(dt_[:, d, :], dt_[:, d, :], ACT.Exp, scale=-1.0))
                    soft.wait(e, c, 3 * d + 2)
                    soft.by(e.activation(dt_[:, d, :], dt_[:, d, :], ACT.Ln, bias=1.0))
                return job

            def spread(s):
                which, g = SPREADS[s]

                def job(c, i):
                    used = Q - GPD + (g + 1) * SG // NG
                    if which == 0:
                        bu_ok.wait(e, c - 1, used)
                    else:
                        last = max(q for q in range(used) if q not in OWN), max(q for q in range(used) if q in OWN)
                        for q in last:
                            wait_ch(e, c - 1, q)
                    for k in range(SG):
                        move("SP", SG * s + k, i, (b_all, c_all)[which][:, SG * g + k, :])
                return job

            def res_on(c, i):
                xs_ok.wait(e, c)
                if has_back(i):
                    wait_full(e, i, "M", NT // 2 - 1)
                sr_ok.by(e.activation(sres[:, :, :], sres_n[:, :, :], ACT.Copy))

            def residual(c, i):
                x1_in.wait(e, c)
                kept_ok.wait(e, c + 1, 1)
                for b in range(NT):
                    x1a_ok.by(e.activation(x1[:, b, :], x1[:, b, :], ACT.Identity,
                                           bias=kept[:, 1, 0, b:b + 1], scale=kept[:, 1, 1, b:b + 1]))

            def normal2(c, i):
                scales2.wait(e, c)
                for b in range(NT):
                    xn2_ok.by(e.activation(xn2[:, b, :], x1[:, b, :], ACT.Identity,
                                           bias=st2[:, 3, b:b + 1], scale=st2[:, 1, b:b + 1]))

            def gate(*fs):
                def job(c, i):
                    for f in fs:
                        move("GATE", f, i, hb[:, f, :])
                return job

            def tails(c, i):
                bank = wait_full(e, i, "TAIL", 0)
                silu_ok.by(e.activation(hb[FR:P, FT, :], bank[0:FR, :], ACT.Copy))
                read_out(e.activation(up_t[FR:P, :], bank[FR:P, :], ACT.Copy), "TAIL", 0)

            def gate_silus(c, i):
                e.preload_act_table(ACT.Silu)
                wait_read(e, i, "TAIL", 0)
                silu_ok.by(e.activation(hb[:, 0:FT, :], hb[:, 0:FT, :], ACT.Silu))
                silu_ok.by(e.activation(hb[FR:P, FT, :], hb[FR:P, FT, :], ACT.Silu))
                e.preload_act_table_set(LOG_EXP)

            table = [(0, "front", turned("XT")), (1, "scan", spread(4)), (2, "front", before_conv(0)), (2, "scan", softplus(ND - 1)),
                     (3, "front", before_conv(1)), (3, "scan", spread(5)), (4, "scan", spread(6)),
                     (5, "front", before_conv(2)), (6, "back", residual), (6, "front", before_conv(3)), (7, "scan", spread(7)),
                     (8, "scan", res_on), (9, "front", res(0)), (12, "back", normal2), (11, "front", res(1, 2)),
                     (13, "front", res(3)), (14, "back", turned("OXT")), (14, "front", front_silus), (15, "back", gate(0, 1)),
                     (15, "back", gate(2, 3)), (17, "back", gate(4)), (18, "back", tails), (18, "back", gate_silus),
                     (20, "front", dt_raw(0)), (20, "front", softplus(0)), (22, "front", dt_raw(1)), (22, "front", softplus(1)),
                     (24, "front", dt_raw(2)), (25, "front", softplus(2)), (25, "next", normal), (28, "front", dt_raw(3)),
                     (29, "front", spread(0)), (30, "front", spread(2)), (31, "front", spread(1)), (31, "front", spread(3))]
            run(e, table, group)

        @block.tensor
        def _(e):
            def product(out_ap, terms):
                for n, (a, b) in enumerate(terms):
                    last = e.matmul(out_ap, a, b, start=(n == 0), stop=(n == len(terms) - 1))
                return last

            def cols(n):
                return slice(n * P, (n + 1) * P)

            e.wait_ge(s_id, POOL_CONSTS)
            e.wait_ge(s_c, DVE_CONSTS)

            def weights_x(c, i):
                e.wait_ge(s_ld[1], 16)
                for j in range(ND):
                    for k in range(ND):
                        last = e.transpose(spare[j][:, cols(k)], wx_ld[:, k, cols(j)], ident[:, :])
                    last.then_inc(s_tr, 1)
                e.wait_ge(s_ld[2], 16)
                e.wait_ge(s_tc, 3 + ND)
                for k in range(ND):
                    product(spare[k][:, :], [(wxT[:, j, cols(k)], wdt_ld[:, j, :]) for j in range(ND)]).then_inc(s_tr, 1)
                e.wait_ge(s_tc, 3 + 2 * ND)
                e.wait_ge(s_ld[4], 16)

            def group(i, q):
                c, q = (i, q - LAG) if q >= LAG else (i - 1, q - LAG + Q)
                if not has_scan(c):
                    return
                if q % GPD == 0:
                    yg_ok.wait(e, c, q // GPD)
                wait_ch(e, c, q)
                y_ok.by(e.matmul(ybank[:, :], ident[:, :], sums[:, q % SUMS, :],
                                 start=(q % GPD == 0), stop=(q % GPD == GPD - 1)))

            def turn(name, src, done):
                def job(c, i):
                    done.wait(e, c)
                    for k in range(KD):
                        bank = wait_free(e, i, name, k)
                        for b in range(NT):
                            last = e.transpose(bank[:, cols(b)], src[:, b, cols(k)], ident[:, :])
                        filled(last, name, k)
                return job

            def project_in(name, d):
                def job(c, i):
                    if (name, d) == ("IN", 0):
                        for k in range(KD):
                            wait_read_before(e, i, "XT", k, ("IN", 0))
                    m = d + (ND if name == "RES" else 0)
                    bank = wait_free(e, i, name, d)
                    filled(product(bank[:, :], [(win[:, k, cols(m)], xT[:, k, :]) for k in range(KD)]), name, d)
                return job

            def convolve(d):
                def job(c, i):
                    wait_read_before(e, i, "IN", d, ("CV", d))
                    bank = wait_free(e, i, "CV", d)
                    filled(product(bank[:, :], [(cdiag[:, d, k, :], xpre[:, d, k:k + TC]) for k in range(TAPS - 1)]), "CV", d)
                return job

            def bc(c, i):
                xs_ok.wait(e, c, ND)
                bank = wait_free(e, i, "BC", 0)
                filled(product(bank[0:3 * W, :], [(wbc[:, k, :, :].rearrange("p r n -> p (r n)"), xs[:, k, :]) for k in range(ND)]), "BC", 0)

            def dt_in(d):
                def job(c, i):
                    bank = wait_free(e, i, "DT", d)
                    filled(product(bank[:, :], [(wc[:, k, cols(d)], xs[:, k, :]) for k in range(ND)]), "DT", d)
                return job

            def spread(s):
                which, g = SPREADS[s]

                def job(c, i):
                    bc_ok.wait(e, c)
                    for k in range(SG):
                        n = which * N + SG * g + k
                        bank = wait_free(e, i, "SP", SG * s + k)
                        filled(e.matmul(bank[:, :], pick[:, n:n + 1].broadcast_to([3 * W, P]), bc_s[:, :], start=True, stop=True),
                               "SP", SG * s + k)
                return job

            def project(t):
                def job(c, i):
                    yg_ok.wait(e, c)
                    bank = wait_free(e, i, "M", t)
                    for b in range(2):
                        last = product(bank[:, b * D:(b + 1) * D], [(sres[:, k, cols(2 * t + b)], wout[:, k, :]) for k in range(ND)])
                    filled(last, "M", t)
                return job

            def expand(name, f):
                def job(c, i):
                    if (name, f) == ("GATE", 0):
                        w13_in.wait(e, c)
                        for k in range(KD):
                            wait_read_before(e, i, "OXT", k, ("GATE", 0))
                    bank = wait_free(e, i, name, f)
                    filled(product(bank[:, :], [(w13[:, k, int(name == "UP"), cols(f)], xT[:, k, :]) for k in range(KD)]), name, f)
                return job

            def tail(c, i):
                bank = wait_free(e, i, "TAIL", 0)
                filled(product(bank[:, :], [(w13t[:, k, :], xT[:, k, :]) for k in range(KD)]), "TAIL", 0)

            def contract(t):
                def job(c, i):
                    w2_in.wait(e, c)
                    tail_ok.wait(e, c)
                    if t == 0:
                        wait_read_before(e, i, "UP", FT - 1, ("DOWN", 0))
                    bank = wait_free(e, i, "DOWN", t)
                    for b in range(2):
                        tok = cols(2 * t + b)
                        last = product(bank[:, b * D:(b + 1) * D], [(hb[:, f, tok], w2s[:, f, :]) for f in range(FT)]
                                       + [(hb[FR:P, FT, tok], w2s[FR:P, FT, :])])
                    filled(last, "DOWN", t)
                return job

            jobs = {"XT": lambda k: turn("XT", xin, xn_ok), "OXT": lambda k: turn("OXT", xn2, xn2_ok), "SP": spread,
                    "IN": lambda d: project_in("IN", d), "RES": lambda d: project_in("RES", d), "M": project, "CV": convolve,
                    "GATE": lambda f: expand("GATE", f), "UP": lambda f: expand("UP", f), "TAIL": lambda k: tail,
                    "BC": lambda k: bc, "DT": dt_in, "DOWN": contract}
            table = [(13, "set-up", weights_x)] + [(at, part, jobs[name](k)) for at, part, name, k in PLAN]
            run(e, table, group, always=True)


_INS = ["L0_attn_x", "L0_attn_rms_w", "L0_attn_W_in", "L0_attn_conv_w", "L0_attn_conv_b", "L0_attn_W_x", "L0_attn_W_dt",
        "L0_attn_A_log", "L0_attn_W_out", "L0_ffn_w1", "L0_ffn_w3", "L0_ffn_w2"]


def kernel(**inputs):
    import numpy as _np
    import concourse.bacc as _bacc
    from concourse import mybir as _mybir
    from concourse.bass_utils import run_bass_kernel_spmd as _run

    nc = _bacc.Bacc("TRN2", target_bir_lowering=False, num_devices=1)
    arrays, args = {}, []
    for name in _INS:
        a = _np.ascontiguousarray(inputs[name])
        arrays[f"in_{name}_dram"] = a
        args.append(nc.dram_tensor(f"in_{name}_dram", a.shape, _mybir.dt.from_np(a.dtype), kind="ExternalInput").ap())
    shape = inputs["L0_attn_x"].shape
    args.append(nc.dram_tensor("out_dram", shape, f32, kind="ExternalOutput").ap())
    mamba_moe_layer(nc, *args)
    r = _run(nc, [arrays], core_ids=[0])
    return r.results[0]["out_dram"]
```
